# Optimizing a Trainium2 kernel written in Bass

```python
import numpy as np
import jax
import jax.numpy as jnp

def _softmax(x, axis=-1):
    return jax.nn.softmax(x, axis=axis)

def _gelu(x):
    return jax.nn.gelu(x, approximate=True)

def _silu(x):
    return jax.nn.silu(x)

def _sigmoid(x):
    return jax.nn.sigmoid(x)

def _layernorm(x, axis=-1, eps=1e-05):
    m = jnp.mean(x, axis=axis, keepdims=True)
    v = jnp.var(x, axis=axis, keepdims=True)
    return (x - m) / jnp.sqrt(v + eps)

def _scatter_add(tgt, idx, src, axis=0):
    return tgt.at[idx].add(src)

def _segment_sum(src, seg, n):
    return jax.ops.segment_sum(src, seg, n)
kernel_name = 'mk_adj_resnorm_d2_adj_r2_2e3fe5'

def setup_inputs(seed: int=0):
    np.random.seed(seed)
    _w = jnp.asarray

    def _rec_inputs():
        import jax
        import jax.numpy as jnp
        _gk = jax.random.key(seed)
        x = 0.0001732 + 1 * jax.random.normal(jax.random.fold_in(_gk, 1), (5120, 64), jnp.float32)
        _w = (1.0 + jnp.arange(5120, dtype=jnp.float32)) ** (-0.5)
        _w = _w / _w.mean()
        _pij = jnp.clip(0.003125 * _w[:, None] * _w[None, :], 0.0, 1.0)
        _a = jax.random.uniform(jax.random.fold_in(_gk, 2), (5120, 5120)) < _pij
        _af = _a.astype(jnp.float32)
        _af = _af * jax.random.uniform(jax.random.fold_in(_gk, 3), (5120, 5120), jnp.float32, 0.05, 0.02)
        adj = _af
        return (x, adj)
    x, adj = _rec_inputs()

    def _L0_gnn_setup():
        import jax, jax.numpy as jnp
        import numpy as np
        N_USERS = 2048
        N_ITEMS = 3072
        EMB = 64
        LN_EPS = 1e-05
        key = jax.random.key(seed)
        ks = jax.random.split(key, 10)
        N = N_USERS + N_ITEMS
        ego = jax.random.normal(ks[0], (N, EMB), jnp.float32)
        adj = (jax.random.uniform(ks[1], (N, N), jnp.float32) < 0.01).astype(jnp.float32) * 0.02
        xav = float(np.sqrt(6.0 / (EMB + EMB)))
        W_u = jax.random.uniform(ks[2], (EMB, EMB), jnp.float32, -xav, xav)
        W_i = jax.random.uniform(ks[3], (EMB, EMB), jnp.float32, -xav, xav)
        diag_u = jax.random.uniform(ks[4], (N_USERS,), jnp.float32, 0.99, 1.01)
        diag_i = jax.random.uniform(ks[5], (N_ITEMS,), jnp.float32, 0.99, 1.01)
        par_u = jax.random.uniform(ks[6], (2,), jnp.float32, 0.0, 0.99)
        par_i = jax.random.uniform(ks[7], (2,), jnp.float32, 0.0, 0.99)
        ln_gamma = jnp.ones((EMB,), jnp.float32)
        ln_beta = jnp.zeros((EMB,), jnp.float32)
        return {'ego_embeddings': ego, 'adj': adj, 'W_u': W_u, 'diag_u': diag_u, 'par_u': par_u, 'W_i': W_i, 'diag_i': diag_i, 'par_i': par_i, 'ln_gamma': ln_gamma, 'ln_beta': ln_beta}
    _L0_gnn_all = _L0_gnn_setup()
    _L0_gnn_in = {k: v for k, v in _L0_gnn_all.items() if k in ('W_u', 'diag_u', 'par_u', 'W_i', 'diag_i', 'par_i', 'ln_gamma', 'ln_beta')}
    del _L0_gnn_all

    def _L1_gnn_setup():
        import jax, jax.numpy as jnp
        import numpy as np
        N, F_IN, F_OUT, K = (8192, 64, 64, 3)
        key = jax.random.key(seed)
        k1, k2, k3, k4 = jax.random.split(key, 4)
        x = jax.random.normal(k1, (N, F_IN), dtype=jnp.float32)
        L_tilde = jax.random.normal(k2, (N, N), dtype=jnp.float32) / np.float32(np.sqrt(N))
        stdv = 1.0 / np.sqrt(F_OUT)
        weights = jax.random.uniform(k3, (K + 1, F_IN, F_OUT), dtype=jnp.float32, minval=-stdv, maxval=stdv)
        bias = jax.random.uniform(k4, (F_OUT,), dtype=jnp.float32, minval=-stdv, maxval=stdv)
        return {'x': x, 'L_tilde': L_tilde, 'weights': weights, 'bias': bias}
    _L1_gnn_all = _L1_gnn_setup()
    _L1_gnn_in = {k: v for k, v in _L1_gnn_all.items() if k in ('weights', 'bias')}
    del _L1_gnn_all
    return {'x': x, 'adj': adj, 'L0_gnn_W_u': _L0_gnn_in['W_u'], 'L0_gnn_diag_u': _L0_gnn_in['diag_u'], 'L0_gnn_par_u': _L0_gnn_in['par_u'], 'L0_gnn_W_i': _L0_gnn_in['W_i'], 'L0_gnn_diag_i': _L0_gnn_in['diag_i'], 'L0_gnn_par_i': _L0_gnn_in['par_i'], 'L0_gnn_ln_gamma': _L0_gnn_in['ln_gamma'], 'L0_gnn_ln_beta': _L0_gnn_in['ln_beta'], 'L1_gnn_weights': _L1_gnn_in['weights'], 'L1_gnn_bias': _L1_gnn_in['bias']}

def reference(x, adj, L0_gnn_W_u, L0_gnn_diag_u, L0_gnn_par_u, L0_gnn_W_i, L0_gnn_diag_i, L0_gnn_par_i, L0_gnn_ln_gamma, L0_gnn_ln_beta, L1_gnn_weights, L1_gnn_bias):
    import jax
    import jax.numpy as jnp

    def _L0_gnn_ref(ego_embeddings, adj, W_u, diag_u, par_u, W_i, diag_i, par_i, ln_gamma, ln_beta):
        import jax, jax.numpy as jnp
        import numpy as np
        N_USERS = 2048
        N_ITEMS = 3072
        EMB = 64
        LN_EPS = 1e-05
        nu = diag_u.shape[0]
        res = ego_embeddings
        ego_u = ego_embeddings[:nu]
        ego_i = ego_embeddings[nu:]
        u = par_u[0] * par_u[1] * (diag_u[:, None] * ego_u @ W_u) + ego_u
        i = par_i[0] * par_i[1] * (diag_i[:, None] * ego_i @ W_i) + ego_i
        e = jnp.concatenate([u, i], axis=0)
        h = adj @ (adj.T @ e)
        mu = jnp.mean(h, axis=-1, keepdims=True)
        var = jnp.var(h, axis=-1, keepdims=True)
        out = (h - mu) * jax.lax.rsqrt(var + LN_EPS) * ln_gamma + ln_beta + res
        return out

    def _L1_gnn_ref(x, L_tilde, weights, bias):
        import jax, jax.numpy as jnp
        import numpy as np
        N, F_IN, F_OUT, K = (8192, 64, 64, 3)
        T_prev = x
        out = T_prev @ weights[0]
        T_curr = L_tilde @ x
        out = out + T_curr @ weights[1]
        for k in range(2, K + 1):
            T_next = 2.0 * (L_tilde @ T_curr) - T_prev
            out = out + T_next @ weights[k]
            T_prev, T_curr = (T_curr, T_next)
        return out + bias
    x = _layernorm(x + _L0_gnn_ref(x, adj, L0_gnn_W_u, L0_gnn_diag_u, L0_gnn_par_u, L0_gnn_W_i, L0_gnn_diag_i, L0_gnn_par_i, L0_gnn_ln_gamma, L0_gnn_ln_beta), axis=-1)
    x = _layernorm(x + _L1_gnn_ref(x, adj, L1_gnn_weights, L1_gnn_bias), axis=-1)
    return x

_drawn_inputs = setup_inputs


def setup_inputs(seed=0):
    import zlib

    import numpy as np

    out = dict(_drawn_inputs(seed))
    spreads = {'L0_gnn_ln_gamma': (1.0, 0.2), 'L0_gnn_ln_beta': (0.0, 0.1)}
    factors = {'L0_gnn_diag_u': 8.0, 'L0_gnn_W_i': 6.07, 'L0_gnn_diag_i': 8.0}
    for name, (base, spread) in spreads.items():
        noise = np.random.default_rng([zlib.crc32(name.encode()), seed]).standard_normal(out[name].shape)
        drawn = base * np.exp(spread * noise) if base else spread * noise
        out[name] = jnp.asarray(drawn.astype(out[name].dtype))
    for name, factor in factors.items():
        out[name] = (out[name] * factor).astype(out[name].dtype)
    return out
```

```python
import numpy as np
import concourse.bass as bass
import concourse.mybir as mybir
from concourse.alu_op_type import AluOpType as ALU

F32 = mybir.dt.float32
ACT = mybir.ActivationFunctionType

N, D = 5120, 64
USERS = 2048
P = 128
BLK = 512
SUB = BLK // P
NB = N // BLK
TILES = N // P
FUSED = 4
PLAIN = NB - FUSED
RING = NB
EPS = 1e-5
LO, HI = slice(0, D), slice(D, 2 * D)


def unit_of(s, i):
    return NB * s + (i if s % 2 == 0 else NB - 1 - i)


def row_of(u):
    return u // NB, (u % NB if (u // NB) % 2 == 0 else NB - 1 - u % NB)


UNITS = 4 * NB


def row_blocks(s, i):
    if s == 0 and i < PLAIN:
        return ([("single", j, LO, -1) for j in range(i, PLAIN)]
                + [("pair", j, None, unit_of(0, j)) for j in range(i)])
    if s == 0:
        return ([("pair", j, None, unit_of(0, j)) for j in range(PLAIN)]
                + [("single", j, HI, unit_of(0, j)) for j in range(PLAIN, i)])
    if s == 1:
        return ([("single", i, HI, unit_of(0, i))]
                + [("pair", j, None, unit_of(1, j)) for j in range(NB - 1, i, -1)])
    if s == 2:
        return ([("single", i, LO, unit_of(1, i))]
                + [("pair", j, None, unit_of(2, j)) for j in range(i)])
    return [("single", j, HI, unit_of(2, j)) for j in range(NB - 1, i - 1, -1)]


def has(kind, u):
    return any(b[0] == kind for b in row_blocks(*row_of(u)))


def stays(j):
    return j == NB - 1


def dve_sums(u):
    return row_of(u) != (3, 0)


def act_sums(u):
    s, i = row_of(u)
    return {0: i >= PLAIN, 1: i < PLAIN + 1, 2: True, 3: True}[s]


def act_saves(u):
    return row_of(u)[0] < 3 and has("pair", u)


def dve_saves(u):
    s, i = row_of(u)
    return s == 0 and i > PLAIN


def upto(flag, u):
    return sum(flag(v) for v in range(u + 1))


def projection(u):
    s, i = row_of(u)
    return {1: 0, 3: NB}[s] + u % NB


TURN = 2 * NB
COLS = NB
ALL_H = FUSED * NB
EACH = SUB // 2


class Steps:

    def __init__(self, eng, sem):
        self.eng, self.sem, self.base, self.n = eng, sem, 0, 0

    def link(self, ins):
        self.n += 1
        ins.then_inc(self.sem, 1)
        self.eng.wait_ge(self.sem, self.base + self.n)


def projections_in(u):
    if u == 2 * NB:
        return [u - 2, u - 1]
    if u == UNITS:
        return [u - 2, u - 1]
    return [u - 2] if NB <= u - 2 < 2 * NB - 2 or 3 * NB <= u - 2 else []


def build(nc, a_nat, a_tr, x, xT, w_u, w_i, diag, par_u, par_i, gamma, beta, bias, weights, out):
    from contextlib import ExitStack
    ctx = ExitStack()
    with ctx:
        def sb(name, shape):
            return ctx.enter_context(nc.sbuf_tensor(name, shape, F32))

        def sem(name):
            return ctx.enter_context(nc.semaphore(name))

        ring = sb("ring", [P, RING, SUB, BLK])
        kept = sb("kept", [P, NB, SUB, BLK])
        ops = sb("ops", [P, TILES, 2 * D])
        acc = sb("acc", [P, TILES, D])
        save = sb("save", [P, NB, BLK])
        sums = sb("sums", [P, 2, BLK])
        tmp = sb("tmp", [P, SUB, D])
        work = sb("work", [P, SUB, D])
        result = sb("result", [P, SUB, D])
        pfused = sb("pfused", [P, SUB, D])
        feat = sb("feat", [P, BLK])
        ident = sb("ident", [P, P])
        w10_sb, w32_sb = sb("w10_sb", [P, D]), sb("w32_sb", [P, D])
        wu_sb, wi_sb = sb("wu_sb", [D, D]), sb("wi_sb", [D, D])
        gamma_sb, beta_sb, bias_sb = sb("gamma_sb", [P, D]), sb("beta_sb", [P, D]), sb("bias_sb", [P, D])
        diag_sb, par_sb, coef = sb("diag_sb", [P, TILES]), sb("par_sb", [P, 4]), sb("coef", [P, 2])
        stats, mv = sb("stats", [P, SUB, 6]), sb("mv", [P, SUB, 2])
        veps, rstd, minus_half = sb("veps", [P, SUB]), sb("rstd", [P, SUB]), sb("minus_half", [P, SUB])
        xT_sb = save[0:D].rearrange("p b c -> p (b c)")

        bank = [ctx.enter_context(nc.psum_tensor(f"bank{n}", [P, BLK], F32)) for n in range(8)]
        PAIR_BANK, TURN_BANK, PROJ_BANK = 4, 6, 7

        loaded = [sem(f"loaded{n}") for n in range(RING)]
        inputs_in = sem("inputs_in")
        const_step = sem("const_step")
        xw_done = sem("xw_done")
        e_ready = sem("e_ready")
        plain_used = sem("plain_used")
        fused_done = sem("fused_done")
        turned_a, turned_d = sem("turned_a"), sem("turned_d")
        kept_a, kept_d = sem("kept_a"), sem("kept_d")
        col_out = sem("col_out")
        col_turned = sem("col_turned")
        col_ready = sem("col_ready")
        h_done = sem("h_done")
        h_saved = sem("h_saved")
        blocks_used = sem("blocks_used")
        row_done = sem("row_done")
        sum_a, sum_d = sem("sum_a"), sem("sum_d")
        saved_a, saved_d = sem("saved_a"), sem("saved_d")
        row_turned = sem("row_turned")
        row_ready = sem("row_ready")
        pair_turned = sem("pair_turned")
        feat_ready = sem("feat_ready")
        proj_done = sem("proj_done")
        proj_used = sem("proj_used")
        var_ready, rstd_ready = sem("var_ready"), sem("rstd_ready")
        dve_step = sem("dve_step")
        result_ready = sem("result_ready")
        stored = sem("stored")

        block = ctx.enter_context(nc.Block())

        INPUTS = 15
        NORMS = 3 * NB

        def slot_of(b, fused):
            return (2 * b + (not fused)) % RING

        @block.sync
        def _(sp):
            def load(slot, src):
                sp.dma_start(ring[:, slot], src).then_inc(loaded[slot], 16)

            def wait_used(q, b, fused):
                if fused:
                    sp.wait_ge(turned_d, EACH * (NB * q + b + 1))
                else:
                    sp.wait_ge(plain_used, NB * q + b + 1)

            back = RING // 2
            def turn(q, first):
                for b in range(NB):
                    for fused in (True, False):
                        if b >= back:
                            wait_used(q, b - back, fused)
                        elif not first:
                            wait_used(q - 1, b + NB - back, fused)
                        col = q + PLAIN if fused else q
                        load(slot_of(b, fused), a_nat[bass.ds(col * NB + b, 1)].rearrange("o p c -> p (o c)")
                             .rearrange("p (a c) -> p a c", a=SUB))

            turn(0, True)
            with sp.Fori(1, FUSED) as q:
                turn(q, False)
            for c in range(FUSED, PLAIN):
                for b in range(NB):
                    if c == FUSED:
                        wait_used(FUSED - 1, NB - back + b // 2, b % 2 == 0)
                    else:
                        wait_used(c - 1, b, False)
                    load(b, a_nat[c * NB + b].rearrange("p (a c) -> p a c", a=SUB))
            gone = []
            for u in range(UNITS):
                s, i = row_of(u)
                row = row_blocks(s, i)
                for m, (kind, j, half, need) in enumerate(row):
                    if stays(j):
                        continue
                    n = len(gone)
                    if n < RING:
                        wait_used(PLAIN - 1, n, False)
                    else:
                        sp.wait_ge(*gone[n - RING])
                    load(n % RING, a_tr[i * NB + j].rearrange("p (a c) -> p a c", a=SUB))
                    done = sum(g[0] is blocks_used for g in gone)
                    gone.append((row_done, u + 1) if m == len(row) - 1 else (blocks_used, done + 1))

        @block.tensor
        def _(pe):
            def single(into, lhs, rhs, first=True, last=True):
                for a in range(SUB):
                    ins = nc.tensor.matmul(bank[into][LO if a % 2 == 0 else HI, :], lhs(a), rhs(a),
                                           start=first and a < 2, stop=last and a >= 2)
                return ins

            def transposes(into, src):
                for a in range(SUB):
                    ins = nc.tensor.transpose(bank[into][:, a * P:(a + 1) * P], src(a), ident[:, :])
                return ins

            pe.wait_ge(inputs_in, 16 * INPUTS)
            for g in range(TILES // 8):
                w = wu_sb if g * 8 * P < USERS else wi_sb
                for t in range(8):
                    tile = g * 8 + t
                    ins = nc.tensor.matmul(bank[g][:, t * D:(t + 1) * D],
                                           xT_sb[:, tile * P:(tile + 1) * P], w[:, :], start=True, stop=True)
                ins.then_inc(xw_done, 1)
            pe.wait_ge(e_ready, TILES // 8)
            pe.wait_ge(const_step, 3)

            def column_block(b, slot, at, into):
                pe.wait_ge(loaded[slot], at)
                return single(into, lambda a: ops[:, SUB * b + a, HI], lambda a: ring[:, slot, a, :],
                              b == 0, b == NB - 1)

            def turn_column(k, which):
                pe.wait_ge(col_out, k + 1)
                transposes(2 + which, lambda a: sums[:, which, a * P:(a + 1) * P]).then_inc(col_turned, 1)

            def add_h(q, b, first):
                if b == 0:
                    pe.wait_ge(col_ready, 2 * q + 1)
                pe.wait_ge(kept_a, EACH * (NB * q + b + 1))
                pe.wait_ge(kept_d, EACH * (NB * q + b + 1))
                if not (first and b < 2):
                    pe.wait_ge(h_saved, NB * q + b - 1)
                single(PAIR_BANK + b % 2, lambda a: pfused[:, a, :],
                       lambda a: kept[:, b, a, :]).then_inc(h_done, 1)

            def turn_block(q, b, slices, first):
                for k in slices:
                    if not (first and b == 0 and k < 2):
                        pe.wait_ge(kept_d if k % 2 else kept_a, EACH * (NB * q + b) + k // 2)
                    transposes(TURN_BANK + k % 2, lambda a: ring[:, slot_of(b, True), a, k * P:(k + 1) * P]
                               ).then_inc(turned_d if k % 2 else turned_a, 1)

            def turn(q, nth):
                first = nth == 0
                for b in range(NB):
                    at = 16 * (2 * q + 2 * b // RING + 1)
                    if b == 0 and not first:
                        pe.wait_ge(col_out, 2 * q)
                    ins = column_block(b, slot_of(b, True), at, 0)
                    if b == NB - 1:
                        ins.then_inc(fused_done, 1)
                    if b and not first:
                        add_h(q - 1, b - 1, nth == 1)
                    if b:
                        turn_block(q, b - 1, (0, 1), first)
                    column_block(b, slot_of(b, False), at, 1).then_inc(plain_used, 1)
                    if b == 0 and not first:
                        turn_column(2 * q - 2, 0)
                        turn_column(2 * q - 1, 1)
                    if b:
                        turn_block(q, b - 1, (2, 3), first)
                if not first:
                    add_h(q - 1, NB - 1, nth == 1)
                turn_block(q, NB - 1, range(SUB), first)

            turn(0, 0)
            turn(1, 1)
            with pe.Fori(2, FUSED) as q:
                turn(q, 2)
            for c in range(FUSED, PLAIN):
                k = FUSED + c
                pe.wait_ge(col_out, k - 1)
                for b in range(NB):
                    at = 16 * (2 * FUSED + c - FUSED + 1)
                    column_block(b, b, at, k % 2).then_inc(plain_used, 1)
                    if b == 0 and c == FUSED:
                        turn_column(k - 2, 0)
                    if b == 0:
                        turn_column(k - 1, (k - 1) % 2)
                    if b and c == FUSED:
                        add_h(FUSED - 1, b - 1, False)
                if c == FUSED:
                    add_h(FUSED - 1, NB - 1, False)

            state = {"n": 0, "ready": 0}

            def need_row(u):
                if u + 1 > state["ready"]:
                    pe.wait_ge(row_ready, u + 1)
                    state["ready"] = u + 1

            def turn_last(u):
                if u == 0:
                    return turn_column(COLS - 1, 1)
                v = u - 1
                pe.wait_ge(sum_d, upto(dve_sums, v))
                pe.wait_ge(sum_a, upto(act_sums, v)) if upto(act_sums, v) else None
                pe.wait_ge(saved_a, upto(act_saves, v)) if upto(act_saves, v) else None
                transposes(v % 4, lambda a: sums[:, v % 2, a * P:(a + 1) * P]).then_inc(row_turned, 1)

            def project_turn(v):
                w, i = projection(v), row_of(v)[1]
                need_row(v)
                if w:
                    pe.wait_ge(feat_ready, w)
                else:
                    pe.wait_ge(kept_a, EACH * ALL_H)
                transposes(TURN_BANK, lambda a: ops[:, SUB * i + a, :]).then_inc(pair_turned, 1)

            def project(v):
                w = projection(v)
                weights = w10_sb if w < NB else w32_sb
                pe.wait_ge(feat_ready, w + 1)
                if w:
                    pe.wait_ge(proj_used, w)
                else:
                    pe.wait_ge(kept_d, EACH * ALL_H)
                for a in range(SUB):
                    ins = nc.tensor.matmul(bank[PROJ_BANK][:, a * D:(a + 1) * D], feat[:, a * P:(a + 1) * P],
                                           weights[:, :], start=True, stop=True)
                ins.then_inc(proj_done, 1)

            for u in range(UNITS):
                s, i = row_of(u)
                row = row_blocks(s, i)
                if u >= 4:
                    need_row(u - 4)
                elif u < 2:
                    pe.wait_ge(col_out, COLS - 1 + u)
                else:
                    pe.wait_ge(col_ready, COLS - 3 + u)
                singles = [m for m, b in enumerate(row) if b[0] == "single"]
                pairs = [m for m, b in enumerate(row) if b[0] == "pair"]
                if pairs:
                    before = [v for v in range(u) if v % 2 == u % 2 and has("pair", v)]
                    if before:
                        v = before[-1]
                        pe.wait_ge(sum_d, upto(dve_sums, v))
                        pe.wait_ge(saved_a, upto(act_saves, v))
                        if upto(dve_saves, v):
                            pe.wait_ge(saved_d, upto(dve_saves, v))
                    else:
                        pe.wait_ge(h_saved, ALL_H)
                turned, project_at = False, None
                for m, (kind, j, half, need) in enumerate(row):
                    if not turned and (m == 1 or need == u - 1):
                        turn_last(u)
                        turned = True
                        todo = projections_in(u)
                        for v in todo[:-1]:
                            project_turn(v)
                            project(v)
                        if todo:
                            project_turn(todo[-1])
                            project_at = m
                    if need >= 0:
                        need_row(need)
                    if s == 0 and kind == "single" and half == LO:
                        pe.wait_ge(col_ready, COLS if j == PLAIN - 1 else COLS - 1)
                    if stays(j):
                        block_of = lambda a: kept[:, i, a, :]
                    else:
                        slot, times = state["n"] % RING, state["n"] // RING
                        pe.wait_ge(loaded[slot], 16 * (NB + times + 1))
                        block_of = lambda a: ring[:, slot, a, :]
                        state["n"] += 1
                    if kind == "single":
                        ins = single(u % 4, lambda a: ops[:, SUB * j + a, half], block_of,
                                     m == singles[0], m == singles[-1])
                    else:
                        for a in range(SUB):
                            ins = nc.tensor.matmul(bank[PAIR_BANK + u % 2][:, :], ops[:, SUB * j + a, :],
                                                   block_of(a), start=m == pairs[0] and a == 0,
                                                   stop=m == pairs[-1] and a == SUB - 1)
                    if m == len(row) - 1:
                        ins.then_inc(row_done, 1)
                    elif not stays(j):
                        ins.then_inc(blocks_used, 1)
                    if project_at == m:
                        project(projections_in(u)[-1])
                        project_at = None
            turn_last(UNITS)
            for v in projections_in(UNITS):
                project_turn(v)
                project(v)

        @block.scalar
        def _(act):
            def bc(v):
                return v.partition_broadcast(P)

            for to, src in ((xT_sb, xT), (wu_sb[:, :], w_u), (wi_sb[:, :], w_i), (acc[:, :, :], x),
                            (diag_sb[:, 0:USERS // P], diag[0]), (diag_sb[:, USERS // P:], diag[1]),
                            (par_sb[:, 0:2], bc(par_u)), (par_sb[:, 2:4], bc(par_i)),
                            (gamma_sb[:, :], bc(gamma)), (beta_sb[:, :], bc(beta)), (bias_sb[:, :], bc(bias)),
                            (w10_sb[LO, :], weights[1]), (w10_sb[HI, :], weights[0]),
                            (w32_sb[LO, :], weights[3]), (w32_sb[HI, :], weights[2])):
                act.dma_start(to, src).then_inc(inputs_in, 16)

            def copy(to, src):
                return nc.scalar.activation(to, src, ACT.Copy)

            def column_out(k, which, done, at):
                act.wait_ge(done, at)
                if not (isinstance(k, int) and k < 2):
                    act.wait_ge(col_turned, k - 1)
                copy(sums[:, which, :], bank[which][:, :]).then_inc(col_out, 1)

            def keep(q, b, k):
                act.wait_ge(turned_a, EACH * (NB * q + b) + k // 2 + 1)
                copy(kept[:, b, k, :], bank[TURN_BANK][:, :]).then_inc(kept_a, 1)

            def turn(q):
                for b in range(NB - 1):
                    if b == NB - 2:
                        column_out(2 * q, 0, fused_done, q + 1)
                    keep(q, b, 0)
                    if b == NB - 2:
                        column_out(2 * q + 1, 1, plain_used, NB * (q + 1))
                    keep(q, b, 2)
                keep(q, NB - 1, 0)
                keep(q, NB - 1, 2)

            act.wait_ge(e_ready, TILES // 8)
            turn(0)
            with act.Fori(1, FUSED) as q:
                turn(q)
            for c in range(FUSED, PLAIN):
                column_out(FUSED + c, (FUSED + c) % 2, plain_used, NB * (c + 1))

            def feats(u):
                for v in projections_in(u):
                    w = projection(v)
                    act.wait_ge(pair_turned, w + 1)
                    if w:
                        act.wait_ge(proj_done, w)
                    copy(feat[:, :], bank[TURN_BANK][:, :]).then_inc(feat_ready, 1)

            def store(v):
                i = row_of(v)[1]
                act.wait_ge(result_ready, projection(v) - NB + 1)
                act.dma_start(out[:, SUB * i:SUB * (i + 1), :], result[:, :, :]).then_inc(stored, 16)

            for u in range(UNITS):
                s, i = row_of(u)
                feats(u)
                if u >= 3 * NB + 3:
                    store(u - 3)
                act.wait_ge(row_done, u + 1)
                if u < 2:
                    act.wait_ge(col_turned, COLS - 1 + u)
                else:
                    act.wait_ge(row_turned, u - 1)
                single_bank, pair_bank = bank[u % 4], bank[PAIR_BANK + u % 2]
                into = sums[:, u % 2, :]
                if act_sums(u):
                    if s == 0:
                        act.wait_ge(h_saved, ALL_H)
                        ins = copy(into[HI], save[HI, i, :])
                    elif s == 1:
                        ins = copy(into[LO], single_bank[LO, :])
                    elif s == 2:
                        ins = copy(into[HI], single_bank[HI, :])
                    elif i:
                        ins = copy(into[LO], single_bank[LO, :])
                    else:
                        ins = copy(into, single_bank[:, :])
                    ins.then_inc(sum_a, 1)
                if act_saves(u):
                    act.wait_ge(sum_d, upto(dve_sums, u))
                    if upto(act_sums, u):
                        act.wait_ge(sum_a, upto(act_sums, u))
                    if dve_saves(u):
                        ins = copy(save[:, i, :], single_bank[:, :])
                    elif s == 1:
                        ins = copy(save[LO, i, :], pair_bank[LO, :])
                    else:
                        ins = copy(save[HI, i, :], pair_bank[HI, :])
                    ins.then_inc(saved_a, 1)
            store(UNITS - 3)
            feats(UNITS)
            store(UNITS - 2)
            store(UNITS - 1)
            act.wait_ge(stored, 16 * NB)

        @block.vector
        def _(dve):
            steps = Steps(dve, dve_step)
            link = steps.link
            add = lambda to, a, b: nc.vector.tensor_tensor(to, a, b, ALU.add)
            mul = lambda to, a, b: nc.vector.tensor_tensor(to, a, b, ALU.mult)

            dve.wait_ge(inputs_in, 16 * INPUTS)
            mul(coef[:, 0:1], par_sb[:, 0:1], par_sb[:, 1:2])
            link(mul(coef[:, 1:2], par_sb[:, 2:3], par_sb[:, 3:4]))
            for n, part in enumerate((diag_sb[:, 0:USERS // P], diag_sb[:, USERS // P:])):
                ins = nc.vector.tensor_scalar(part, part, coef[:, n:n + 1], None, ALU.mult)
            link(ins)
            for g in range(TILES // 8):
                part = slice(8 * g, 8 * g + 8)
                scaled = sums[:, g % 2, :].rearrange("p (t d) -> p t d", d=D)
                dve.wait_ge(xw_done, g + 1)
                link(mul(scaled, bank[g][:, :].rearrange("p (t d) -> p t d", d=D),
                         diag_sb[:, part].unsqueeze(2).to_broadcast([P, 8, D])))
                add(ops[:, part, HI], scaled, acc[:, part, :]).then_inc(e_ready, 1)

            def halves(n):
                v = bank[n][:, :].rearrange("p (a f) -> p a f", f=2 * D)
                return v[:, :, LO], v[:, :, HI]

            def fold_column(k, which, col, fused):
                dve.wait_ge(col_turned, k + 1)
                low, high = halves(2 + which)
                link(nc.vector.tensor_copy(tmp[:, :, :], high))
                if fused:
                    add(pfused[:, :, :], low, tmp[:, :, :])
                add(ops[:, bass.ds(SUB * col, SUB), LO], low, tmp[:, :, :]).then_inc(col_ready, 1)
                dve.wait_ge(col_ready, k + 1)

            def save_h(q, b, first):
                dve.wait_ge(h_done, NB * q + b + 1)
                share = bank[PAIR_BANK + b % 2][:, :]
                if first:
                    ins = nc.vector.tensor_copy(save[:, b, :], share)
                else:
                    dve.wait_ge(h_saved, NB * (q - 1) + b + 1)
                    ins = add(save[:, b, :], share, save[:, b, :])
                ins.then_inc(h_saved, 1)

            def keep(q, b, k):
                dve.wait_ge(turned_d, EACH * (NB * q + b) + k // 2 + 1)
                nc.vector.tensor_copy(kept[:, b, k, :], bank[TURN_BANK + 1][:, :]).then_inc(kept_d, 1)

            def turn(q, nth):
                for b in range(NB):
                    if b == 0 and nth:
                        fold_column(2 * q - 2, 0, PLAIN + q - 1, True)
                        fold_column(2 * q - 1, 1, q - 1, False)
                    if b:
                        if nth:
                            save_h(q - 1, b - 1, nth == 1)
                        keep(q, b - 1, 1)
                        keep(q, b - 1, 3)
                if nth:
                    save_h(q - 1, NB - 1, nth == 1)
                keep(q, NB - 1, 1)
                keep(q, NB - 1, 3)

            turn(0, 0)
            turn(1, 1)
            done, per = steps.n, 2
            with dve.Fori(2, FUSED) as q:
                steps.base, steps.n = done + per * (q - 2), 0
                turn(q, 2)
                assert steps.n == per
            steps.base, steps.n = 0, done + per * (FUSED - 2)
            fold_column(2 * FUSED - 2, 0, NB - 1, True)
            fold_column(2 * FUSED - 1, 1, FUSED - 1, False)
            for b in range(NB):
                save_h(FUSED - 1, b, False)
            for c in range(FUSED, PLAIN):
                fold_column(FUSED + c, (FUSED + c) % 2, c, False)

            def over_rows(v):
                return v[:, :].unsqueeze(1).to_broadcast([P, SUB, D])

            norms = 0

            def norm(to, src):
                nonlocal norms
                norms += 1
                for a in range(SUB):
                    ins = nc.vector.bn_stats(stats[:, a, :], src[:, a, :])
                link(ins)
                for a in range(SUB):
                    ins = nc.vector.bn_aggr(mv[:, a, :], stats[:, a, :])
                link(ins)
                nc.vector.tensor_scalar(veps[:, :], mv[:, :, 1], EPS, None, ALU.add).then_inc(var_ready, 1)
                dve.wait_ge(rstd_ready, norms)
                for a in range(SUB):
                    ins = nc.vector.tensor_scalar(to[:, a, :], src[:, a, :], mv[:, a, 0:1], rstd[:, a:a + 1],
                                                  ALU.subtract, ALU.mult)
                return ins

            def use_projection(v):
                w, i = projection(v), row_of(v)[1]
                rows = slice(SUB * i, SUB * (i + 1))
                product = bank[PROJ_BANK][:, 0:SUB * D].rearrange("p (a d) -> p a d", d=D)
                dve.wait_ge(proj_done, w + 1)
                if w < NB:
                    link(add(acc[:, rows, :], product, over_rows(bias_sb)))
                    add(acc[:, rows, :], acc[:, rows, :], ops[:, rows, HI]).then_inc(proj_used, 1)
                    dve.wait_ge(proj_used, w + 1)
                else:
                    if w > NB:
                        dve.wait_ge(result_ready, w - NB)
                    add(work[:, :, :], product, acc[:, rows, :]).then_inc(proj_used, 1)
                    dve.wait_ge(proj_used, w + 1)
                    if w > NB:
                        dve.wait_ge(stored, 16 * (w - NB))
                    norm(result, work).then_inc(result_ready, 1)

            for u in range(UNITS):
                s, i = row_of(u)
                rows = slice(SUB * i, SUB * (i + 1))
                dve.wait_ge(row_done, u + 1)
                if u < 2:
                    dve.wait_ge(col_turned, COLS - 1 + u)
                else:
                    dve.wait_ge(row_turned, u - 1)
                single_bank, pair_bank = bank[u % 4], bank[PAIR_BANK + u % 2]
                into = sums[:, u % 2, :]
                if dve_sums(u):
                    end = (LO, HI, LO, HI)[s]
                    part = slice(0, P) if s == 0 and i < PLAIN or s == 1 and i > PLAIN else end
                    if s == 0:
                        dve.wait_ge(h_saved, ALL_H)
                        found = True
                        first = pair_bank[LO, :] if i >= PLAIN else single_bank[:, :]
                    else:
                        found = (s == 1 and i > 0) or (s == 2 and i < NB - 1) or s == 3
                        first = single_bank[part, :]
                        if found:
                            dve.wait_ge(saved_a, upto(act_saves, unit_of(s - 1, i)))
                            if s == 1 and i > PLAIN:
                                dve.wait_ge(saved_d, upto(dve_saves, unit_of(s - 1, i)))
                    if found:
                        ins = add(into[part], first, save[part, i, :])
                    else:
                        ins = nc.vector.tensor_copy(into[part], first)
                    if has("pair", u) and not (s == 0 and i >= PLAIN):
                        link(ins)
                        ins = add(into[end], pair_bank[end, :], into[end])
                    ins.then_inc(sum_d, 1)
                if dve_saves(u):
                    dve.wait_ge(saved_a, upto(act_saves, u))
                    add(save[HI, i, :], pair_bank[HI, :], save[HI, i, :]).then_inc(saved_d, 1)
                dve.wait_ge(row_turned, u + 1)
                low, high = halves(u % 4)
                link(nc.vector.tensor_copy(tmp[:, :, :], high))
                if s == 1:
                    add(ops[:, rows, LO], low, tmp[:, :, :]).then_inc(row_ready, 1)
                else:
                    link(add(work[:, :, :], low, tmp[:, :, :]))
                if s == 0:
                    w_ = work[:, :, :]
                    link(norm(w_, w_))
                    link(mul(w_, w_, over_rows(gamma_sb)))
                    link(add(w_, w_, over_rows(beta_sb)))
                    link(add(w_, w_, acc[:, rows, :]))
                    link(add(w_, w_, acc[:, rows, :]))
                    norm(ops[:, rows, HI], w_).then_inc(row_ready, 1)
                elif s > 1:
                    was = HI if s == 2 else LO
                    nc.vector.scalar_tensor_tensor(ops[:, rows, was], work[:, :, :], 2.0, ops[:, rows, was],
                                                   ALU.mult, ALU.subtract).then_inc(row_ready, 1)
                dve.wait_ge(row_ready, u + 1)
                for v in projections_in(u + 1):
                    use_projection(v)

        @block.gpsimd
        def _(pool):
            nc.gpsimd.memset(minus_half[:, :], -0.5).then_inc(const_step, 1)
            nc.gpsimd.memset(ident[:, :], 0.0).then_inc(const_step, 1)
            pool.wait_ge(const_step, 2)
            nc.gpsimd.affine_select(out=ident[:, :], in_=ident[:, :], compare_op=ALU.not_equal, fill=1.0,
                                    base=0, pattern=[[-1, P]], channel_multiplier=1).then_inc(const_step, 1)
            with pool.Fori(0, NORMS) as n:
                pool.wait_ge(var_ready, n + 1)
                nc.gpsimd.tensor_tensor(rstd[:, :], veps[:, :], minus_half[:, :], ALU.pow).then_inc(rstd_ready, 1)


def kernel(x, adj, L0_gnn_W_u, L0_gnn_diag_u, L0_gnn_par_u, L0_gnn_W_i, L0_gnn_diag_i, L0_gnn_par_i,
           L0_gnn_ln_gamma, L0_gnn_ln_beta, L1_gnn_weights, L1_gnn_bias):
    import concourse.bacc as bacc
    from concourse.bass_utils import run_bass_kernel_spmd

    nc = bacc.Bacc("TRN2", target_bir_lowering=False, num_devices=1, dynamic_dma_scratch_size=1024)
    lay = np.ascontiguousarray
    x, adj = np.asarray(x), np.asarray(adj)

    def blocks(m):
        return lay(m.reshape(NB, SUB, P, NB, BLK).transpose(3, 0, 2, 1, 4)).reshape(NB * NB, P, SUB * BLK)

    def by_partition(v):
        return lay(v.reshape(-1, P).T)

    arrays = {
        "a_nat": blocks(adj), "a_tr": blocks(adj.T),
        "x": lay(x.reshape(TILES, P, D).transpose(1, 0, 2)), "xT": lay(x.T),
        "w_u": lay(L0_gnn_W_u), "w_i": lay(L0_gnn_W_i),
        "diag_u": by_partition(np.asarray(L0_gnn_diag_u)), "diag_i": by_partition(np.asarray(L0_gnn_diag_i)),
        "par_u": lay(L0_gnn_par_u), "par_i": lay(L0_gnn_par_i),
        "gamma": lay(L0_gnn_ln_gamma), "beta": lay(L0_gnn_ln_beta),
        "bias": lay(L1_gnn_bias), "weights": lay(L1_gnn_weights),
    }
    t = {name: nc.dram_tensor(name, a.shape, F32, kind="ExternalInput").ap() for name, a in arrays.items()}
    out = nc.dram_tensor("out", (P, TILES, D), F32, kind="ExternalOutput").ap()
    build(nc, t["a_nat"], t["a_tr"], t["x"], t["xT"], t["w_u"], t["w_i"], (t["diag_u"], t["diag_i"]),
          t["par_u"], t["par_i"], t["gamma"], t["beta"], t["bias"], t["weights"], out)
    r = run_bass_kernel_spmd(nc, [arrays], core_ids=[0])
    return lay(r.results[0]["out"].transpose(1, 0, 2)).reshape(N, D)
```

```python
import numpy as np
import concourse.bass as bass
import concourse.mybir as mybir
from concourse.alu_op_type import AluOpType as ALU

F32 = mybir.dt.float32
ACT = mybir.ActivationFunctionType

N, D = 5120, 64
USERS = 2048
P = 128
BLK = 512
SUB = BLK // P
NB = N // BLK
TILES = N // P
FUSED = 3
PLAIN = NB - FUSED
RING = NB
EPS = 1e-5
LO, HI = slice(0, D), slice(D, 2 * D)


def unit_of(s, i):
    return NB * s + (i if s % 2 == 0 else NB - 1 - i)


def row_of(u):
    return u // NB, (u % NB if (u // NB) % 2 == 0 else NB - 1 - u % NB)


UNITS = 4 * NB


def row_blocks(s, i):
    if s == 0 and i < PLAIN:
        return ([("single", j, LO, -1) for j in range(i, PLAIN)]
                + [("pair", j, None, unit_of(0, j)) for j in range(i)])
    if s == 0:
        return [("pair", j, None, unit_of(0, j)) for j in range(PLAIN)]
    if s == 1:
        return ([("single", j, HI, unit_of(0, j)) for j in range(min(PLAIN, i), i + 1)]
                + [("pair", j, None, unit_of(1, j)) for j in range(NB - 1, i, -1)])
    if s == 2:
        return ([("single", i, LO, unit_of(1, i))]
                + [("pair", j, None, unit_of(2, j)) for j in range(i)])
    js = list(range(NB - 1, i - 1, -1))
    if i == NB - 2:
        js.reverse()
    return [("single", j, HI, unit_of(2, j)) for j in js]


AHEAD = {NB: [(NB, 0), (NB, 1), (NB + 1, 0), (NB + 1, 1), (NB + 2, 0)],
         2 * NB: [(2 * NB + 1, 0), (2 * NB + 2, 0)],
         3 * NB: [(3 * NB + 1, 0)]}
EARLY = [block for blocks in AHEAD.values() for block in blocks]


def sweep_order():
    for u in range(UNITS):
        row = row_blocks(*row_of(u))
        own = [m for m in range(len(row)) if (u, m) not in EARLY]
        work = [("block", *block) for block in AHEAD.get(u, [])]
        at_once = not work and row[own[0]][3] == u - 1
        work += [("block", u, m) for m in own]
        work.insert(0 if at_once else 1, ("turn", u, 0))
        yield from work


def has(kind, u):
    return any(b[0] == kind for b in row_blocks(*row_of(u)))


def stays(j):
    return j == NB - 1


def dve_sums(u):
    return row_of(u) != (3, 0)


def act_sums(u):
    s, i = row_of(u)
    return s > 0 or i >= PLAIN


def act_saves(u):
    return row_of(u)[0] < 3 and has("pair", u)


def upto(flag, u):
    return sum(flag(v) for v in range(u + 1))


def projection(u):
    return u - NB


def projections_in(u):
    if u == 2 * NB:
        return [u - 2, u - 1]
    return [u - 2] if NB <= u - 2 < 2 * NB - 2 else []


LANES = 3
LAST = PLAIN - 1
assert PLAIN == 2 * FUSED + 1
COLS = NB
ALL_H = FUSED * NB
ALL_PLAIN = 2 * NB * FUSED
EACH = SUB // 2
ZEROED = 2


class Steps:

    def __init__(self, eng, sem):
        self.eng, self.sem, self.base, self.n = eng, sem, 0, 0

    def link(self, ins):
        self.n += 1
        ins.then_inc(self.sem, 1)
        self.eng.wait_ge(self.sem, self.base + self.n)


def build(nc, a_nat, a_tr, x, xT, diag, rows, weights, out):
    from contextlib import ExitStack
    ctx = ExitStack()
    with ctx:
        def sb(name, shape):
            return ctx.enter_context(nc.sbuf_tensor(name, shape, F32))

        def sem(name):
            return ctx.enter_context(nc.semaphore(name))

        ring = sb("ring", [P, RING, SUB, BLK])
        kept = sb("kept", [P, NB, SUB, BLK])
        ops = sb("ops", [P, TILES, 2 * D])
        acc = sb("acc", [P, TILES, D])
        save = sb("save", [P, NB, BLK])
        sums = sb("sums", [P, 2, BLK])
        tmp = sb("tmp", [P, SUB, D])
        work = sb("work", [P, SUB, D])
        pfused = sb("pfused", [P, SUB, D])
        result = pfused
        feat = sb("feat", [P, BLK])
        ident = sb("ident", [P, P])
        w_pair = sb("w_pair", [P, 2 * D])
        w_z = sb("w_z", [P, 2 * D])
        w_w = sb("w_w", [P, 2 * D])
        rows_sb = sb("rows_sb", [P, 3 * D + 4])
        gamma_sb, beta_sb, bias_sb = (rows_sb[:, n * D:(n + 1) * D] for n in range(3))
        par_sb = rows_sb[:, 3 * D:]
        diag_sb, coef = sb("diag_sb", [P, TILES]), sb("coef", [P, 2])
        stats, mv = sb("stats", [P, SUB, 6]), sb("mv", [P, SUB, 2])
        veps, rstd, minus_half = sb("veps", [P, SUB]), sb("rstd", [P, SUB]), sb("minus_half", [P, SUB])
        xT_sb = save[:, 0:NB // 2, :].rearrange("p b c -> p (b c)")
        w_in = feat[:, 0:6 * D]
        w_ui, w10_in, w32_in, w22_in, w33_in = (w_in[:, a * D:b * D] for a, b in (
            (0, 2), (2, 3), (3, 4), (4, 5), (5, 6)))

        bank = [ctx.enter_context(nc.psum_tensor(f"bank{n}", [P, BLK], F32)) for n in range(8)]
        PAIR_BANK, TURN_BANK, PROJ_BANK = 4, 6, 7
        COL_BANK = 3

        def single_bank_of(u):
            return (u + 1) % 4

        def column_sum(lane):
            return feat[:, :] if lane == 2 else sums[:, lane, :]

        loaded = [sem(f"loaded{n}") for n in range(RING)]
        xT_in, x_in = sem("xT_in"), sem("x_in")
        inputs_in = sem("inputs_in")
        weights_ready = sem("weights_ready")
        const_step = sem("const_step")
        xw_done = sem("xw_done")
        e_ready = sem("e_ready")
        plain_used = sem("plain_used")
        fused_done = sem("fused_done")
        turned_a, turned_d = sem("turned_a"), sem("turned_d")
        kept_a, kept_d = sem("kept_a"), sem("kept_d")
        col_out = sem("col_out")
        col_turned = sem("col_turned")
        col_ready = sem("col_ready")
        h_done = sem("h_done")
        h_saved = sem("h_saved")
        blocks_used = sem("blocks_used")
        row_done = sem("row_done")
        sum_a, sum_d = sem("sum_a"), sem("sum_d")
        saved = sem("saved")
        row_turned = sem("row_turned")
        row_ready = sem("row_ready")
        pair_turned = sem("pair_turned")
        feat_ready = sem("feat_ready")
        proj_done = sem("proj_done")
        proj_used = sem("proj_used")
        var_ready, rstd_ready = sem("var_ready"), sem("rstd_ready")
        dve_step = sem("dve_step")
        result_ready = sem("result_ready")
        stored = sem("stored")

        block = ctx.enter_context(nc.Block())

        INPUTS = 3
        NORMS = 3 * NB
        GROUPS = TILES // SUB // 2

        def slot_of(b, lane):
            return (LANES * b + lane) % RING

        def loads_of(q, b, lane):
            return LANES * NB // RING * q + (LANES * b + lane) // RING + 1

        def plain_count(q, b, lane):
            return 2 * NB * q + 2 * b + lane

        @block.sync
        def _(sp):
            def load(slot, src):
                sp.dma_start(ring[:, slot], src).then_inc(loaded[slot], 16)

            def wait_used(q, m):
                b, lane = m // LANES, m % LANES
                if lane:
                    sp.wait_ge(plain_used, plain_count(q, b, lane))
                else:
                    sp.wait_ge(turned_d, EACH * (NB * q + b + 1))

            def turn(q, first):
                for m in range(LANES * NB):
                    b, lane = m // LANES, m % LANES
                    if m >= RING:
                        wait_used(q, m - RING)
                    elif not first:
                        wait_used(q - 1, m + LANES * NB - RING)
                    col = 2 * q + lane - 1 if lane else q + PLAIN
                    load(slot_of(b, lane), a_nat[bass.ds(col * NB + b, 1)].rearrange("o p c -> p (o c)")
                         .rearrange("p (a c) -> p a c", a=SUB))

            sp.dma_start(w_in, weights).then_inc(inputs_in, 16)
            sp.dma_start(diag_sb[:, :], diag).then_inc(inputs_in, 16)
            sp.dma_start(rows_sb[:, :], rows.partition_broadcast(P)).then_inc(inputs_in, 16)
            sp.dma_start(xT_sb, xT).then_inc(xT_in, 16)
            sp.dma_start(acc[:, :, :], x).then_inc(x_in, 16)
            turn(0, True)
            with sp.Fori(1, FUSED) as q:
                turn(q, False)
            for b in range(NB):
                wait_used(FUSED - 1, LANES * NB - RING + b)
                load(b, a_nat[LAST * NB + b].rearrange("p (a c) -> p a c", a=SUB))
            gone = []
            counted = 0
            for what, u, m in sweep_order():
                i, row = row_of(u)[1], row_blocks(*row_of(u))
                j = row[m][1]
                if what == "turn" or stays(j):
                    continue
                n = len(gone)
                if n < RING:
                    sp.wait_ge(plain_used, ALL_PLAIN + n + 1)
                else:
                    sp.wait_ge(*gone[n - RING])
                load(n % RING, a_tr[i * NB + j].rearrange("p (a c) -> p a c", a=SUB))
                if m == len(row) - 1:
                    gone.append((row_done, u + 1))
                else:
                    counted += 1
                    gone.append((blocks_used, counted))

        @block.tensor
        def _(pe):
            def single(into, lhs, rhs, first=True, last=True):
                for a in range(SUB):
                    ins = nc.tensor.matmul(bank[into][LO if a % 2 == 0 else HI, :], lhs(a), rhs(a),
                                           start=first and a < 2, stop=last and a >= 2)
                return ins

            def transposes(into, src):
                for a in range(SUB):
                    ins = nc.tensor.transpose(bank[into][:, a * P:(a + 1) * P], src(a), ident[:, :])
                return ins

            pe.wait_ge(xT_in, 16)
            pe.wait_ge(inputs_in, 16 * INPUTS)
            for g in range(GROUPS):
                if g >= 4:
                    pe.wait_ge(e_ready, 2 * (g - 3))
                for a in range(SUB):
                    t = SUB * g + a
                    for n, half in enumerate((LO, HI)):
                        ins = nc.tensor.matmul(bank[2 * (g % 4) + n][:, a * P:(a + 1) * P],
                                               xT_sb[half, t * P:(t + 1) * P], w_ui[half, :],
                                               start=True, stop=True)
                ins.then_inc(xw_done, 1)
            pe.wait_ge(e_ready, 2 * GROUPS)
            pe.wait_ge(const_step, 3)

            def column_block(b, slot, at, into):
                pe.wait_ge(loaded[slot], at)
                return single(into, lambda a: ops[:, SUB * b + a, HI], lambda a: ring[:, slot, a, :],
                              b == 0, b == NB - 1)

            def turn_column(k, lane, first):
                pe.wait_ge(col_out, k + 1)
                if not first:
                    pe.wait_ge(col_ready, k)
                transposes(COL_BANK, lambda a: column_sum(lane)[:, a * P:(a + 1) * P]).then_inc(col_turned, 1)

            def add_h(q, b):
                if b == 0:
                    pe.wait_ge(col_ready, LANES * q + 1)
                pe.wait_ge(kept_a, EACH * (NB * q + b + 1))
                pe.wait_ge(kept_d, EACH * (NB * q + b + 1))
                pe.wait_ge(h_saved, ZEROED + NB * q + b - 1)
                single(PAIR_BANK + b % 2, lambda a: pfused[:, a, :],
                       lambda a: kept[:, b, a, :]).then_inc(h_done, 1)

            def turn_block(q, b, slices, first):
                for k in slices:
                    if not (first and b == 0 and k < 2):
                        pe.wait_ge(kept_d if k % 2 else kept_a, EACH * (NB * q + b) + k // 2)
                    transposes(TURN_BANK + k % 2, lambda a: ring[:, slot_of(b, 0), a, k * P:(k + 1) * P]
                               ).then_inc(turned_d if k % 2 else turned_a, 1)

            def turn(q, first):
                for b in range(NB):
                    if b == 0 and not first:
                        pe.wait_ge(col_out, LANES * q)
                    for lane in range(LANES):
                        ins = column_block(b, slot_of(b, lane), 16 * loads_of(q, b, lane), lane)
                        if lane:
                            ins.then_inc(plain_used, 1)
                        elif b == NB - 1:
                            ins.then_inc(fused_done, 1)
                        if b == 0 and not first:
                            turn_column(LANES * (q - 1) + lane, lane, lane == 0 and isinstance(q, int))
                        if b and lane == 0 and not first:
                            add_h(q - 1, b - 1)
                        if b and lane < 2:
                            turn_block(q, b - 1, (2 * lane, 2 * lane + 1), first)
                if not first:
                    add_h(q - 1, NB - 1)
                turn_block(q, NB - 1, range(SUB), first)

            turn(0, True)
            with pe.Fori(1, FUSED) as q:
                turn(q, False)
            for b in range(NB):
                column_block(b, b, 16 * (LANES * FUSED + 1), 0).then_inc(plain_used, 1)
                if b < LANES:
                    turn_column(LANES * (FUSED - 1) + b, b, False)
                if b:
                    add_h(FUSED - 1, b - 1)
            add_h(FUSED - 1, NB - 1)

            state = {"n": 0, "ready": 0}

            def need_row(u):
                if u + 1 > state["ready"]:
                    pe.wait_ge(row_ready, u + 1)
                    state["ready"] = u + 1

            def turn_last(u):
                if u == 0:
                    return turn_column(COLS - 1, 0, False)
                v = u - 1
                into = single_bank_of(v)
                pe.wait_ge(sum_d, upto(dve_sums, v))
                if upto(act_sums, v):
                    pe.wait_ge(sum_a, upto(act_sums, v))
                if v < 2 * NB:
                    ins = transposes(into, lambda a: sums[:, v % 2, a * P:(a + 1) * P])
                else:
                    if v == 2 * NB:
                        pe.wait_ge(weights_ready, 1)
                    for a in range(SUB):
                        ins = nc.tensor.matmul(bank[into][:, a * P:(a + 1) * P],
                                               sums[:, v % 2, a * P:(a + 1) * P],
                                               (w_z if v < 3 * NB else w_w)[:, :], start=True, stop=True)
                ins.then_inc(row_turned, 1)

            def project_turn(v):
                w, i = projection(v), row_of(v)[1]
                need_row(v)
                if w:
                    pe.wait_ge(feat_ready, w)
                else:
                    pe.wait_ge(kept_a, EACH * ALL_H)
                transposes(TURN_BANK, lambda a: ops[:, SUB * i + a, :]).then_inc(pair_turned, 1)

            def project(v):
                w = projection(v)
                if w == 0:
                    pe.wait_ge(weights_ready, 1)
                pe.wait_ge(feat_ready, w + 1)
                if w:
                    pe.wait_ge(proj_used, w)
                else:
                    pe.wait_ge(kept_d, EACH * ALL_H)
                for a in range(SUB):
                    ins = nc.tensor.matmul(bank[PROJ_BANK][:, a * P:(a + 1) * P], feat[:, a * P:(a + 1) * P],
                                           w_pair[:, :], start=True, stop=True)
                ins.then_inc(proj_done, 1)

            begun, project_now = set(), []
            for what, u, m in sweep_order():
                s, i = row_of(u)
                row = row_blocks(s, i)
                if what == "turn":
                    turn_last(u)
                    project_now = projections_in(u)
                    for v in project_now[:-1]:
                        project_turn(v)
                        project(v)
                    if project_now:
                        project_turn(project_now[-1])
                    continue
                kind, j, half, need = row[m]
                singles = [m for m, b in enumerate(row) if b[0] == "single"]
                pairs = [m for m, b in enumerate(row) if b[0] == "pair"]
                if u not in begun:
                    begun.add(u)
                    if u >= 4:
                        need_row(u - 4)
                    elif u == 2:
                        pe.wait_ge(col_ready, COLS)
                    else:
                        pe.wait_ge(col_out, COLS)
                if pairs and m == pairs[0]:
                    before = [v for v in range(u) if v % 2 == u % 2 and has("pair", v)]
                    if before:
                        pe.wait_ge(sum_d, upto(dve_sums, before[-1]))
                        pe.wait_ge(saved, upto(act_saves, before[-1]))
                    else:
                        pe.wait_ge(h_saved, ZEROED + ALL_H)
                if need >= 0:
                    need_row(need)
                if s == 0 and kind == "single":
                    pe.wait_ge(col_ready, COLS if j == LAST else COLS - 1)
                if stays(j):
                    block_of = lambda a: kept[:, i, a, :]
                else:
                    slot, times = state["n"] % RING, state["n"] // RING
                    pe.wait_ge(loaded[slot], 16 * (NB + times + 1))
                    block_of = lambda a: ring[:, slot, a, :]
                    state["n"] += 1
                if kind == "single":
                    ins = single(single_bank_of(u), lambda a: ops[:, SUB * j + a, half], block_of,
                                 m == singles[0], m == singles[-1])
                else:
                    for a in range(SUB):
                        ins = nc.tensor.matmul(bank[PAIR_BANK + u % 2][:, :], ops[:, SUB * j + a, :],
                                               block_of(a), start=m == pairs[0] and a == 0,
                                               stop=m == pairs[-1] and a == SUB - 1)
                if m == len(row) - 1:
                    ins.then_inc(row_done, 1)
                elif not stays(j):
                    ins.then_inc(blocks_used, 1)
                if project_now:
                    project(project_now[-1])
                    project_now = []
            turn_last(UNITS)

        @block.scalar
        def _(act):
            def copy(to, src):
                return nc.scalar.activation(to, src, ACT.Copy)

            def column_out(k, lane, done, at, first=False):
                act.wait_ge(done, at)
                if not first:
                    act.wait_ge(col_turned, k - LANES + 1)
                copy(column_sum(lane), bank[lane][:, :]).then_inc(col_out, 1)

            def keep(q, b, k):
                act.wait_ge(turned_a, EACH * (NB * q + b) + k // 2 + 1)
                copy(kept[:, b, k, :], bank[TURN_BANK][:, :]).then_inc(kept_a, 1)

            def turn(q, first):
                for b in range(NB - 1):
                    if b == NB - 2:
                        column_out(LANES * q, 0, fused_done, q + 1, first)
                    keep(q, b, 0)
                    if b == NB - 2:
                        column_out(LANES * q + 1, 1, plain_used, plain_count(q, NB - 1, 1), first)
                    keep(q, b, 2)
                column_out(LANES * q + 2, 2, plain_used, plain_count(q, NB - 1, 2), first)
                keep(q, NB - 1, 0)
                keep(q, NB - 1, 2)

            act.wait_ge(weights_ready, 1)
            turn(0, True)
            with act.Fori(1, FUSED) as q:
                turn(q, False)
            column_out(COLS - 1, 0, plain_used, ALL_PLAIN + NB)

            def feats(u):
                for v in projections_in(u):
                    w = projection(v)
                    act.wait_ge(pair_turned, w + 1)
                    if w:
                        act.wait_ge(proj_done, w)
                    copy(feat[:, :], bank[TURN_BANK][:, :]).then_inc(feat_ready, 1)

            def store(v):
                i = row_of(v)[1]
                act.wait_ge(result_ready, v - 3 * NB + 1)
                act.dma_start(out[:, SUB * i:SUB * (i + 1), :], result[:, :, :]).then_inc(stored, 16)

            for u in range(UNITS):
                s, i = row_of(u)
                feats(u)
                if u >= 3 * NB + 2:
                    store(u - 2)
                act.wait_ge(row_done, u + 1)
                if u < 2:
                    act.wait_ge(col_turned, COLS)
                else:
                    act.wait_ge(row_turned, u - 1)
                single_bank, pair_bank = bank[single_bank_of(u)], bank[PAIR_BANK + u % 2]
                into = sums[:, u % 2, :]
                if act_sums(u):
                    if s == 0:
                        act.wait_ge(h_saved, ZEROED + ALL_H)
                        ins = copy(into[HI], save[HI, i, :])
                    elif s == 1:
                        ins = copy(into[LO], single_bank[LO, :])
                    elif s == 2:
                        ins = copy(into[HI], single_bank[HI, :])
                    elif i:
                        ins = copy(into[LO], single_bank[LO, :])
                    else:
                        ins = copy(into, single_bank[:, :])
                    ins.then_inc(sum_a, 1)
                if act_saves(u):
                    act.wait_ge(sum_d, upto(dve_sums, u))
                    if upto(act_sums, u):
                        act.wait_ge(sum_a, upto(act_sums, u))
                    half = LO if s == 1 else HI
                    copy(save[half, i, :], pair_bank[half, :]).then_inc(saved, 1)
            store(UNITS - 2)
            store(UNITS - 1)
            act.wait_ge(stored, 16 * NB)

        @block.vector
        def _(dve):
            steps = Steps(dve, dve_step)
            link = steps.link
            add = lambda to, a, b: nc.vector.tensor_tensor(to, a, b, ALU.add)
            mul = lambda to, a, b: nc.vector.tensor_tensor(to, a, b, ALU.mult)

            def over_rows(v, n=SUB):
                return v.unsqueeze(1).to_broadcast([P, n, D])

            dve.wait_ge(inputs_in, 16 * INPUTS)
            mul(coef[:, 0:1], par_sb[:, 0:1], par_sb[:, 1:2])
            link(mul(coef[:, 1:2], par_sb[:, 2:3], par_sb[:, 3:4]))
            for n, part in enumerate((diag_sb[:, 0:USERS // P], diag_sb[:, USERS // P:])):
                ins = nc.vector.tensor_scalar(part, part, coef[:, n:n + 1], None, ALU.mult)
            link(ins)
            dve.wait_ge(x_in, 16)
            for g in range(GROUPS):
                dve.wait_ge(xw_done, g + 1)
                for n in range(2):
                    at = SUB * (g + GROUPS * n)
                    part = slice(at, at + SUB)
                    product = bank[2 * (g % 4) + n][:, :].rearrange("p (a f) -> p a f", f=2 * D)
                    link(mul(work[:, :, :], product[:, :, LO if at * P < USERS else HI],
                             diag_sb[:, part].unsqueeze(2).to_broadcast([P, SUB, D])))
                    add(ops[:, part, HI], work[:, :, :], acc[:, part, :]).then_inc(e_ready, 1)
                    dve.wait_ge(e_ready, 2 * g + n + 1)
            nc.vector.scalar_tensor_tensor(acc[:, :, :], acc[:, :, :], 2.0, over_rows(beta_sb, TILES),
                                           ALU.mult, ALU.add)
            dve.wait_ge(const_step, 3)
            for half in (LO, HI):
                nc.vector.tensor_tensor(w_pair[:, half], w10_in, w32_in, ALU.subtract)
                nc.vector.tensor_scalar(w_w[:, half], w33_in, 2.0, None, ALU.mult)
            nc.vector.tensor_scalar(w_z[:, HI], w22_in, 2.0, None, ALU.mult)
            add(w_z[:, LO], ident[:, LO], ident[:, HI]).then_inc(weights_ready, 1)

            def halves(n):
                v = bank[n][:, :].rearrange("p (a f) -> p a f", f=2 * D)
                return v[:, :, LO], v[:, :, HI]

            def fold_column(k, col, fused):
                dve.wait_ge(col_turned, k + 1)
                low, high = halves(COL_BANK)
                link(nc.vector.tensor_copy(tmp[:, :, :], high))
                if fused:
                    add(pfused[:, :, :], low, tmp[:, :, :])
                add(ops[:, bass.ds(SUB * col, SUB), LO], low, tmp[:, :, :]).then_inc(col_ready, 1)
                dve.wait_ge(col_ready, k + 1)

            def save_h(q, b):
                dve.wait_ge(h_done, NB * q + b + 1)
                dve.wait_ge(h_saved, ZEROED + NB * q + b)
                add(save[:, b, :], bank[PAIR_BANK + b % 2][:, :], save[:, b, :]).then_inc(h_saved, 1)

            def keep(q, b, k):
                dve.wait_ge(turned_d, EACH * (NB * q + b) + k // 2 + 1)
                nc.vector.tensor_copy(kept[:, b, k, :], bank[TURN_BANK + 1][:, :]).then_inc(kept_d, 1)

            def turn(q, first):
                for b in range(NB):
                    if b == 0 and not first:
                        for lane in range(LANES):
                            fold_column(LANES * (q - 1) + lane, 2 * (q - 1) + lane - 1 if lane else
                                        PLAIN + q - 1, lane == 0)
                    if b:
                        if not first:
                            save_h(q - 1, b - 1)
                        keep(q, b - 1, 1)
                        keep(q, b - 1, 3)
                if not first:
                    save_h(q - 1, NB - 1)
                keep(q, NB - 1, 1)
                keep(q, NB - 1, 3)

            turn(0, True)
            done, per = steps.n, LANES
            with dve.Fori(1, FUSED) as q:
                steps.base, steps.n = done + per * (q - 1), 0
                turn(q, False)
                assert steps.n == per
            steps.base, steps.n = 0, done + per * (FUSED - 1)
            for b in range(NB):
                if b < LANES:
                    q = FUSED - 1
                    fold_column(LANES * q + b, 2 * q + b - 1 if b else PLAIN + q, b == 0)
                if b:
                    save_h(FUSED - 1, b - 1)
            save_h(FUSED - 1, NB - 1)
            fold_column(COLS - 1, LAST, False)

            norms = 0

            def norm(to, src):
                nonlocal norms
                norms += 1
                for a in range(SUB):
                    ins = nc.vector.bn_stats(stats[:, a, :], src[:, a, :])
                link(ins)
                for a in range(SUB):
                    ins = nc.vector.bn_aggr(mv[:, a, :], stats[:, a, :])
                link(ins)
                nc.vector.tensor_scalar(veps[:, :], mv[:, :, 1], EPS, None, ALU.add).then_inc(var_ready, 1)
                dve.wait_ge(rstd_ready, norms)
                for a in range(SUB):
                    ins = nc.vector.tensor_scalar(to[:, a, :], src[:, a, :], mv[:, a, 0:1], rstd[:, a:a + 1],
                                                  ALU.subtract, ALU.mult)
                return ins

            def use_projection(v):
                w, i = projection(v), row_of(v)[1]
                rows = slice(SUB * i, SUB * (i + 1))
                dve.wait_ge(proj_done, w + 1)
                link(add(acc[:, rows, :], halves(PROJ_BANK)[0], over_rows(bias_sb)))
                add(acc[:, rows, :], acc[:, rows, :], ops[:, rows, HI]).then_inc(proj_used, 1)
                dve.wait_ge(proj_used, w + 1)

            for u in range(UNITS):
                s, i = row_of(u)
                rows = slice(SUB * i, SUB * (i + 1))
                dve.wait_ge(row_done, u + 1)
                if u < 2:
                    dve.wait_ge(col_turned, COLS)
                else:
                    dve.wait_ge(row_turned, u - 1)
                single_bank, pair_bank = bank[single_bank_of(u)], bank[PAIR_BANK + u % 2]
                into = sums[:, u % 2, :]
                if dve_sums(u):
                    end = (LO, HI, LO, HI)[s]
                    part = slice(0, P) if s == 0 and i < PLAIN else end
                    if s == 0:
                        dve.wait_ge(h_saved, ZEROED + ALL_H)
                        found = True
                        first = pair_bank[LO, :] if i >= PLAIN else single_bank[:, :]
                    else:
                        found = (s == 1 and i > 0) or (s == 2 and i < NB - 1) or s == 3
                        first = single_bank[part, :]
                        if found:
                            dve.wait_ge(saved, upto(act_saves, unit_of(s - 1, i)))
                    if found:
                        ins = add(into[part], first, save[part, i, :])
                    else:
                        ins = nc.vector.tensor_copy(into[part], first)
                    if has("pair", u) and not (s == 0 and i >= PLAIN):
                        link(ins)
                        ins = add(into[end], pair_bank[end, :], into[end])
                    ins.then_inc(sum_d, 1)
                dve.wait_ge(row_turned, u + 1)
                low, high = halves(single_bank_of(u))
                t0, sum_of = ops[:, rows, HI], acc[:, rows, :]
                if s < 2:
                    link(nc.vector.tensor_copy(tmp[:, :, :], high))
                if s == 0:
                    v = work[:, :, :]
                    link(add(v, low, tmp[:, :, :]))
                    link(norm(v, v))
                    link(mul(v, v, over_rows(gamma_sb)))
                    link(add(v, v, sum_of))
                    norm(t0, v).then_inc(row_ready, 1)
                elif s == 1:
                    add(ops[:, rows, LO], low, tmp[:, :, :]).then_inc(row_ready, 1)
                elif s == 2:
                    add(sum_of, high, sum_of)
                    nc.vector.scalar_tensor_tensor(t0, low, 2.0, t0, ALU.mult, ALU.subtract
                                                   ).then_inc(row_ready, 1)
                else:
                    add(work[:, :, :], high, sum_of).then_inc(row_ready, 1)
                    if u > 3 * NB:
                        dve.wait_ge(stored, 16 * (u - 3 * NB))
                dve.wait_ge(row_ready, u + 1)
                if s == 3:
                    norm(result, work).then_inc(result_ready, 1)
                    dve.wait_ge(result_ready, u - 3 * NB + 1)
                for v in projections_in(u + 1):
                    use_projection(v)

        @block.gpsimd
        def _(pool):
            nc.gpsimd.memset(minus_half[:, :], -0.5).then_inc(const_step, 1)
            nc.gpsimd.memset(ident[:, :], 0.0).then_inc(const_step, 1)
            pool.wait_ge(const_step, 2)
            nc.gpsimd.affine_select(out=ident[:, :], in_=ident[:, :], compare_op=ALU.not_equal, fill=1.0,
                                    base=0, pattern=[[-1, P]], channel_multiplier=1).then_inc(const_step, 1)
            pool.wait_ge(xw_done, GROUPS)
            for part in (slice(0, NB // 2), slice(NB // 2, NB)):
                nc.gpsimd.memset(save[:, part, :], 0.0).then_inc(h_saved, 1)
            with pool.Fori(0, NORMS) as n:
                pool.wait_ge(var_ready, n + 1)
                nc.gpsimd.tensor_tensor(rstd[:, :], veps[:, :], minus_half[:, :], ALU.pow).then_inc(rstd_ready, 1)


def kernel(x, adj, L0_gnn_W_u, L0_gnn_diag_u, L0_gnn_par_u, L0_gnn_W_i, L0_gnn_diag_i, L0_gnn_par_i,
           L0_gnn_ln_gamma, L0_gnn_ln_beta, L1_gnn_weights, L1_gnn_bias):
    import concourse.bacc as bacc
    from concourse.bass_utils import run_bass_kernel_spmd

    nc = bacc.Bacc("TRN2", target_bir_lowering=False, num_devices=1, dynamic_dma_scratch_size=1024)
    lay = np.ascontiguousarray
    x, adj, W_u, W_i, W = (np.asarray(v) for v in (x, adj, L0_gnn_W_u, L0_gnn_W_i, L1_gnn_weights))

    def blocks(m):
        return lay(m.reshape(NB, SUB, P, NB, BLK).transpose(3, 0, 2, 1, 4)).reshape(NB * NB, P, SUB * BLK)

    def by_partition(v):
        return lay(v.reshape(-1, P).T)

    arrays = {
        "a_nat": blocks(adj), "a_tr": blocks(adj.T),
        "x": lay(x.reshape(TILES, P, D).transpose(1, 0, 2)), "xT": lay(x.reshape(2, N // 2, D).transpose(0, 2, 1)).reshape(P, N // 2),
        "diag": by_partition(np.concatenate([L0_gnn_diag_u, L0_gnn_diag_i])),
        "rows": np.concatenate([L0_gnn_ln_gamma, L0_gnn_ln_beta, L1_gnn_bias, L0_gnn_par_u, L0_gnn_par_i]),
        "weights": lay(np.concatenate([np.concatenate(over) for over in (
            (W_u, W_u), (W_i, W_i), (W[1], W[0]), (W[3], W[2]), (W[2], W[2]), (W[3], W[3]))], axis=1)),
    }
    t = {name: nc.dram_tensor(name, a.shape, F32, kind="ExternalInput").ap() for name, a in arrays.items()}
    out = nc.dram_tensor("out", (P, TILES, D), F32, kind="ExternalOutput").ap()
    build(nc, t["a_nat"], t["a_tr"], t["x"], t["xT"], t["diag"], t["rows"], t["weights"], out)
    r = run_bass_kernel_spmd(nc, [arrays], core_ids=[0])
    return lay(r.results[0]["out"].transpose(1, 0, 2)).reshape(N, D)
```

```python
import numpy as np
import concourse.bass as bass
import concourse.mybir as mybir
from concourse.alu_op_type import AluOpType as ALU

F32 = mybir.dt.float32
ACT = mybir.ActivationFunctionType

N, D = 5120, 64
USERS = 2048
P = 128
BLK = 512
SUB = BLK // P
NB = N // BLK
TILES = N // P
FUSED = 5
PLAIN = NB - FUSED
RING = NB
EPS = 1e-5
LO, HI = slice(0, D), slice(D, 2 * D)


def unit_of(s, i):
    return NB * s + (i if s % 2 == 0 else NB - 1 - i)


def row_of(u):
    return u // NB, (u % NB if (u // NB) % 2 == 0 else NB - 1 - u % NB)


UNITS = 4 * NB


def row_blocks(s, i):
    if s == 0 and i < PLAIN:
        return ([("single", j, LO, -1) for j in range(i, PLAIN)]
                + [("pair", j, None, unit_of(0, j)) for j in range(i)])
    if s == 0:
        return [("pair", j, None, unit_of(0, j)) for j in range(PLAIN)]
    if s == 1:
        return ([("single", j, HI, unit_of(0, j)) for j in range(min(PLAIN, i), i + 1)]
                + [("pair", j, None, unit_of(1, j)) for j in range(NB - 1, i, -1)])
    if s == 2:
        return ([("single", i, LO, unit_of(1, i))]
                + [("pair", j, None, unit_of(2, j)) for j in range(i)])
    js = list(range(NB - 1, i - 1, -1))
    if i in (NB - 2, NB - 3):
        js.reverse()
    return [("single", j, HI, unit_of(2, j)) for j in js]


AHEAD = {NB: [(NB, 0), (NB, 1), (NB, 2), (NB + 1, 0), (NB + 1, 1), (NB + 1, 2)],
         2 * NB: [(2 * NB + 1, 0), (2 * NB + 2, 0)],
         3 * NB: [(3 * NB + 1, 0), (3 * NB + 2, 0), (3 * NB + 2, 1)]}
EARLY = [block for blocks in AHEAD.values() for block in blocks]


def sweep_order():
    for u in range(UNITS):
        row = row_blocks(*row_of(u))
        own = [m for m in range(len(row)) if (u, m) not in EARLY]
        work = [("block", *block) for block in AHEAD.get(u, [])]
        at_once = not work and row[own[0]][3] == u - 1
        work += [("block", u, m) for m in own]
        if u == 3 * NB + 3:
            work.insert(2, ("turn", u - 1, 0))
            work.append(("turn", u, 0))
        elif u > 3 * NB + 3:
            work.insert(3, ("turn", u, 0))
        elif u != 3 * NB + 2:
            work.insert(0 if at_once else 1, ("turn", u, 0))
        yield from work


def has(kind, u):
    return any(b[0] == kind for b in row_blocks(*row_of(u)))


def stays(j):
    return j == NB - 1


STAY = 3
HELD = {(unit_of(s + 1, i), [b[1] for b in row_blocks(s + 1, i)].index(i)): (unit_of(s, i), 0)
        for s in (1, 2) for i in (range(STAY) if s == 1 else range(NB - 1 - STAY, NB - 1))}
assert all(row_blocks(*row_of(u))[m][1] == row_of(u)[1] for pair in HELD.items() for u, m in pair)


def ring_places():
    places, freed, had, n = {}, list(range(RING)), [0] * RING, 0
    for what, u, m in sweep_order():
        if what == "turn" or stays(row_blocks(*row_of(u))[m][1]):
            continue
        if (u, m) in HELD:
            places[u, m] = places[HELD[u, m]]
        else:
            had[freed[n]] += 1
            places[u, m] = freed[n], had[freed[n]]
            n += 1
        if (u, m) not in HELD.values():
            freed.append(places[u, m][0])
    return places


def dve_sums(u):
    return row_of(u) != (3, 0)


def act_sums(u):
    s, i = row_of(u)
    return s > 0 or i >= PLAIN


def act_saves(u):
    return row_of(u)[0] < 3 and has("pair", u)


def upto(flag, u):
    return sum(flag(v) for v in range(u + 1))


def both(u):
    return has("single", u) and has("pair", u)


PROJECTIONS = {**{u: [u - 2] for u in range(NB + 2, 2 * NB - 1)},
               2 * NB: [2 * NB - 3, 2 * NB - 1], 2 * NB + 1: [2 * NB - 2]}
PROJECTION_ORDER = [v for vs in PROJECTIONS.values() for v in vs]
assert sorted(PROJECTION_ORDER) == list(range(NB, 2 * NB))


def projection(v):
    return PROJECTION_ORDER.index(v)


def projections_in(u):
    return PROJECTIONS.get(u, [])


LANES = 2
LEFT = tuple(range(FUSED - 1, PLAIN))
COLS = NB
ALL_PLAIN = NB * (FUSED - 1)
ALL_OUT = 1 + LANES * (FUSED - 1)
LAST_H = (("left", 1), ("left", 3), ("left", 5), ("left", 7), ("left", 9),
          (0, 1), (0, 2), (0, 3), (1, 1), (2, 1))
assert len(LEFT) == 1 and len(LAST_H) == NB
ALL_H = FUSED * NB


TWIN = 1


def by_pe(b):
    return b % 2 == 1 and b != TWIN


def by_pe_first(b):
    return b % 4 != 0


PE_FIRST = sum(by_pe_first(b) for b in range(NB))
PE_TURN = sum(by_pe(b) for b in range(NB))


def h_before(i):
    return ZEROED + (FUSED - 1) * NB + i + 1


ZEROED = 2


class Steps:

    def __init__(self, eng, sem):
        self.eng, self.sem, self.base, self.n = eng, sem, 0, 0

    def link(self, ins):
        self.n += 1
        ins.then_inc(self.sem, 1)
        self.eng.wait_ge(self.sem, self.base + self.n)


def build(nc, a_nat, a_tr, x, xT, diag, rows, weights, out):
    from contextlib import ExitStack
    ctx = ExitStack()
    with ctx:
        def sb(name, shape):
            return ctx.enter_context(nc.sbuf_tensor(name, shape, F32))

        def sem(name):
            return ctx.enter_context(nc.semaphore(name))

        ring = sb("ring", [P, RING, SUB, BLK])
        kept = sb("kept", [P, NB, SUB, BLK])
        ops = sb("ops", [P, TILES, 2 * D])
        acc = sb("acc", [P, TILES, D])
        save = sb("save", [P, NB, BLK])
        sums = sb("sums", [P, 2, BLK])
        tmp = sb("tmp", [P, SUB, D])
        work = sb("work", [P, SUB, D])
        pfused = sb("pfused", [P, SUB, D])
        result = (pfused, tmp)
        feat = sb("feat", [P, BLK])
        ident = sb("ident", [P, P])
        w_pair = sb("w_pair", [P, 2 * D])
        w_z = sb("w_z", [P, 2 * D])
        w_w = sb("w_w", [P, 2 * D])
        rows_sb = sb("rows_sb", [P, 3 * D + 4])
        gamma_sb, beta_sb, bias_sb = (rows_sb[:, n * D:(n + 1) * D] for n in range(3))
        par_sb = rows_sb[:, 3 * D:]
        diag_sb, coef = sb("diag_sb", [P, TILES]), sb("coef", [P, 2])
        stats, mv = sb("stats", [P, SUB, 6]), sb("mv", [P, SUB, 2])
        veps, rstd, minus_half = sb("veps", [P, SUB]), sb("rstd", [P, SUB]), sb("minus_half", [P, SUB])
        xT_sb = save[:, 0:NB // 2, :].rearrange("p b c -> p (b c)")
        w_in = feat[:, 0:8 * D]
        w_ui, w_ii, w10_in, w32_in, w22_in, w33_in = (w_in[:, a * D:b * D] for a, b in (
            (0, 2), (2, 4), (4, 5), (5, 6), (6, 7), (7, 8)))

        bank = [ctx.enter_context(nc.psum_tensor(f"bank{n}", [P, BLK], F32)) for n in range(8)]
        PAIR_BANK, TURN_BANK, PROJ_BANK = 4, 6, 7
        COL_BANK = 3

        def single_bank_of(u):
            return (u + 2) % 4

        loaded = [sem(f"loaded{n}") for n in range(RING)]
        xT_in = [sem(f"xT_in{n}") for n in range(2)]
        x_in = [sem(f"x_in{n}") for n in range(2)]
        inputs_in = sem("inputs_in")
        weights_ready = sem("weights_ready")
        const_step = sem("const_step")
        xw_done = sem("xw_done")
        e_ready = sem("e_ready")
        plain_used = sem("plain_used")
        fused_done = sem("fused_done")
        slice_turned = sem("slice_turned")
        slice_kept = sem("slice_kept")
        block_kept = sem("block_kept")
        twin_in = sem("twin_in")
        col_out = sem("col_out")
        col_turned = sem("col_turned")
        col_ready = sem("col_ready")
        h_done = sem("h_done")
        h_saved = sem("h_saved")
        blocks_used = sem("blocks_used")
        singles_done = sem("singles_done")
        row_done = sem("row_done")
        sum_a, sum_d = sem("sum_a"), sem("sum_d")
        saved = sem("saved")
        row_turned = sem("row_turned")
        row_ready = sem("row_ready")
        pair_turned = sem("pair_turned")
        feat_ready = sem("feat_ready")
        proj_done = sem("proj_done")
        proj_used = sem("proj_used")
        var_ready, rstd_ready = sem("var_ready"), sem("rstd_ready")
        dve_step = sem("dve_step")
        result_ready = sem("result_ready")
        stored = [sem(f"stored{n}") for n in range(2)]

        places = ring_places()
        block = ctx.enter_context(nc.Block())

        INPUTS = 3
        NORMS = 3 * NB
        GROUPS = TILES // SUB // 2

        def group_bank(g):
            return 1 + g

        def slot_of(b, lane):
            return (LANES * b + lane) % RING

        def loads_of(q, b, lane):
            return 1 + LANES * NB // RING * (q - 1) + (LANES * b + lane) // RING + 1

        def plain_count(q, b):
            return NB * (q - 1) + b + 1

        def turned_before(q, b):
            if by_pe(b):
                return PE_FIRST + PE_TURN * (q - 1) + sum(by_pe(n) for n in range(b))
            return NB - PE_FIRST + NB // 2 * (q - 1) + b // 2

        def turned_before_first(b):
            return sum(by_pe_first(n) == by_pe_first(b) for n in range(b))

        def turned_count(q, lane):
            return LANES * q + lane

        PARTS = (slice(0, SUB), slice(SUB, TILES // 2))
        x_half = x.rearrange("p (h t) d -> p h t d", h=2)
        acc_half = acc[:, :, :].rearrange("p (h t) d -> p h t d", h=2)

        @block.sync
        def _(sp):
            def load(slot, src):
                sp.dma_start(ring[:, slot], src).then_inc(loaded[slot], 16)

            def block_at(a, at):
                return a[bass.ds(at, 1)].rearrange("o p c -> p (o c)").rearrange("p (a c) -> p a c", a=SUB)

            def wait_used(q, m):
                b, lane = m // LANES, m % LANES
                if lane or b == TWIN:
                    sp.wait_ge(plain_used, plain_count(q, b))
                elif by_pe(b):
                    sp.wait_ge(slice_turned, SUB * (turned_before(q, b) + 1))
                else:
                    sp.wait_ge(block_kept, turned_before(q, b) + 1)

            def half_turn(q, half):
                for m in range(RING * half, RING * half + RING):
                    b, lane = m // LANES, m % LANES
                    if half:
                        wait_used(q, m - RING)
                    elif isinstance(q, int):
                        if by_pe_first(m):
                            sp.wait_ge(slice_turned, SUB * (turned_before_first(m) + 1))
                        else:
                            sp.wait_ge(block_kept, turned_before_first(m) + 1)
                            sp.wait_ge(slice_turned, SUB * (turned_before_first(m + 1) + 1))
                    else:
                        wait_used(q - 1, m + RING)
                    col = (q + PLAIN, q - 1)[lane]
                    load(slot_of(b, lane), block_at(a_nat, col * NB + b))
                if half:
                    sp.wait_ge(h_done, NB * (q - 1) + TWIN + 1)
                    sp.dma_start(kept[:, TWIN], block_at(a_tr, TWIN * NB + PLAIN + q)).then_inc(twin_in, 16)

            sp.dma_start(w_in, weights).then_inc(inputs_in, 16)
            sp.dma_start(diag_sb[:, :], diag).then_inc(inputs_in, 16)
            sp.dma_start(rows_sb[:, :], rows.partition_broadcast(P)).then_inc(inputs_in, 16)
            for n, part in enumerate(PARTS):
                nodes = slice(part.start * P, part.stop * P)
                sp.dma_start(xT_sb[:, nodes], xT[:, nodes]).then_inc(xT_in[n], 16)
                sp.dma_start(acc_half[:, :, part], x_half[:, :, part]).then_inc(x_in[n], 16)
                for b in ((0,) if n == 0 else range(1, NB)):
                    load(b, a_nat[PLAIN * NB + b].rearrange("p (a c) -> p a c", a=SUB))
            half_turn(1, 0)
            with sp.Fori(1, FUSED - 1) as q:
                half_turn(q, 1)
                half_turn(q + 1, 0)
            half_turn(FUSED - 1, 1)
            for col in LEFT:
                for b in range(NB):
                    wait_used(FUSED - 1, LANES * NB - RING + b)
                    load(b, a_nat[col * NB + b].rearrange("p (a c) -> p a c", a=SUB))
            gone = [(plain_used, ALL_PLAIN + n + 1) for n in range(RING)]
            counted, n = 0, 0
            for what, u, m in sweep_order():
                i, row = row_of(u)[1], row_blocks(*row_of(u))
                j = row[m][1]
                if what == "turn" or stays(j):
                    continue
                if (u, m) not in HELD:
                    sp.wait_ge(*gone[n])
                    load(places[u, m][0], a_tr[i * NB + j].rearrange("p (a c) -> p a c", a=SUB))
                    n += 1
                if m == len(row) - 1:
                    used = (row_done, u + 1)
                elif both(u) and row[m][0] == "single" and row[m + 1][0] == "pair":
                    used = (singles_done, upto(both, u))
                else:
                    counted += 1
                    used = (blocks_used, counted)
                if (u, m) not in HELD.values():
                    gone.append(used)

        @block.tensor
        def _(pe):
            def single(into, lhs, rhs, first=True, last=True):
                for a in range(SUB):
                    ins = nc.tensor.matmul(bank[into][LO if a % 2 == 0 else HI, :], lhs(a), rhs(a),
                                           start=first and a < 2, stop=last and a >= 2)
                return ins

            def transposes(into, src):
                for a in range(SUB):
                    ins = nc.tensor.transpose(bank[into][:, a * P:(a + 1) * P], src(a), ident[:, :])
                return ins

            pe.wait_ge(inputs_in, 16 * INPUTS)

            def x_products(groups):
                for g in groups:
                    if g < 2:
                        pe.wait_ge(xT_in[g], 16)
                    for a in range(SUB):
                        t = SUB * g + a
                        ins = nc.tensor.matmul(bank[group_bank(g)][:, a * P:(a + 1) * P],
                                               xT_sb[:, t * P:(t + 1) * P], w_ui if t * P < USERS else w_ii,
                                               start=True, stop=True)
                    ins.then_inc(xw_done, 1)

            x_products(range(1))

            def column_block(b, slot, at, into):
                pe.wait_ge(loaded[slot], at)
                return single(into, lambda a: ops[:, SUB * b + a, HI], lambda a: ring[:, slot, a, :],
                              b == 0, b == NB - 1)

            def turn_column(count, lane, first=False):
                pe.wait_ge(col_out, count)
                if not first:
                    pe.wait_ge(col_ready, count - 1)
                transposes(COL_BANK, lambda a: sums[:, lane, a * P:(a + 1) * P]).then_inc(col_turned, 1)

            def add_h(q, b, into=PAIR_BANK):
                if b == 0:
                    pe.wait_ge(col_ready, turned_count(q + 1, 0) - 1)
                    pe.wait_ge(slice_kept, SUB * turned_before(q + 1, TWIN + 2))
                if b in (0, NB - 2):
                    pe.wait_ge(block_kept, turned_before(q + 1, 0) - (1 if b == 0 else 0))
                pe.wait_ge(h_saved, ZEROED + NB * q + b - 1)
                single(into + b % 2, lambda a: pfused[:, a, :],
                       lambda a: kept[:, b, a, :]).then_inc(h_done, 1)

            def turn_block(b, slot, before, slices, first):
                for k in slices:
                    if not (first and before + k < 2):
                        pe.wait_ge(slice_kept, before + k - 1)
                    transposes(TURN_BANK + k % 2, lambda a: ring[:, slot, a, k * P:(k + 1) * P]
                               ).then_inc(slice_turned, 1)

            for b in range(NB):
                if b < GROUPS:
                    pe.wait_ge(e_ready, 2 * b + 1)
                elif b == GROUPS:
                    pe.wait_ge(e_ready, 2 * GROUPS)
                if b == 1:
                    pe.wait_ge(const_step, 3)
                ins = column_block(b, b, 16, 0)
                if b == NB - 1:
                    ins.then_inc(fused_done, 1)
                if b and by_pe_first(b - 1):
                    turn_block(b - 1, b - 1, SUB * turned_before_first(b - 1), (2, 3), True)
                if b == 0:
                    x_products(range(1, GROUPS))
                if by_pe_first(b):
                    turn_block(b, b, SUB * turned_before_first(b), (0, 1), True)
            turn_block(b, b, SUB * turned_before_first(b), (2, 3), True)
            turn_column(1, 0, first=True)

            def turn(q):
                pe.wait_ge(col_out, turned_count(q, 0) - 1)
                for b in range(NB):
                    for lane in range(LANES):
                        ins = column_block(b, slot_of(b, lane), 16 * loads_of(q, b, lane), lane)
                        if lane:
                            ins.then_inc(plain_used, 1)
                        elif b == NB - 1:
                            ins.then_inc(fused_done, 1)
                        if b and lane == 0:
                            add_h(q - 1, b - 1)
                        if b and by_pe(b - 1):
                            turn_block(b - 1, slot_of(b - 1, 0), SUB * turned_before(q, b - 1),
                                       (2 * lane, 2 * lane + 1), False)
                add_h(q - 1, NB - 1)
                pe.wait_ge(twin_in, 16 * q)
                turn_column(turned_count(q, 0), 0)
                turn_block(NB - 1, slot_of(NB - 1, 0), SUB * turned_before(q, NB - 1), range(SUB), False)
                turn_column(turned_count(q, 1), 1)

            with pe.Fori(1, FUSED) as q:
                turn(q)
            pe.wait_ge(col_out, ALL_OUT)
            for b in range(NB):
                column_block(b, b, 16 * loads_of(FUSED, 0, 0), 0).then_inc(plain_used, 1)
                if ("left", b) in LAST_H:
                    add_h(FUSED - 1, LAST_H.index(("left", b)), TURN_BANK)

            state = {"ready": 0}

            def need_row(u):
                if u + 1 > state["ready"]:
                    pe.wait_ge(row_ready, u + 1)
                    state["ready"] = u + 1

            def turn_last(u):
                if u == 0:
                    return turn_column(COLS, 0)
                v = u - 1
                into = single_bank_of(v)
                pe.wait_ge(sum_d, upto(dve_sums, v))
                if upto(act_sums, v):
                    pe.wait_ge(sum_a, upto(act_sums, v))
                if v < 2 * NB:
                    ins = transposes(into, lambda a: sums[:, v % 2, a * P:(a + 1) * P])
                else:
                    if v == 2 * NB:
                        pe.wait_ge(weights_ready, 2)
                    for a in range(SUB):
                        ins = nc.tensor.matmul(bank[into][:, a * P:(a + 1) * P],
                                               sums[:, v % 2, a * P:(a + 1) * P],
                                               (w_z if v < 3 * NB else w_w)[:, :], start=True, stop=True)
                ins.then_inc(row_turned, 1)

            def project_turn(v):
                w, i = projection(v), row_of(v)[1]
                need_row(v)
                if w:
                    pe.wait_ge(feat_ready, w)
                else:
                    pe.wait_ge(h_saved, ZEROED + ALL_H)
                transposes(TURN_BANK, lambda a: ops[:, SUB * i + a, :]).then_inc(pair_turned, 1)

            def project(v):
                w = projection(v)
                if w == 0:
                    pe.wait_ge(weights_ready, 2)
                pe.wait_ge(feat_ready, w + 1)
                if w:
                    pe.wait_ge(proj_used, w)
                else:
                    pe.wait_ge(h_saved, ZEROED + ALL_H)
                for a in range(SUB):
                    ins = nc.tensor.matmul(bank[PROJ_BANK][:, a * P:(a + 1) * P], feat[:, a * P:(a + 1) * P],
                                           w_pair[:, :], start=True, stop=True)
                ins.then_inc(proj_done, 1)

            begun, project_now = set(), []
            for what, u, m in sweep_order():
                s, i = row_of(u)
                row = row_blocks(s, i)
                if what == "turn":
                    turn_last(u)
                    project_now = projections_in(u)
                    for v in project_now[:-1]:
                        project_turn(v)
                        project(v)
                    if project_now:
                        project_turn(project_now[-1])
                    continue
                kind, j, half, need = row[m]
                singles = [m for m, b in enumerate(row) if b[0] == "single"]
                pairs = [m for m, b in enumerate(row) if b[0] == "pair"]
                if u not in begun:
                    begun.add(u)
                    if u >= 4:
                        need_row(u - 4)
                    elif u == 1:
                        pe.wait_ge(col_ready, COLS)
                    elif u:
                        pe.wait_ge(col_out, COLS)
                if pairs and m == pairs[0]:
                    before = [v for v in range(u) if v % 2 == u % 2 and has("pair", v)]
                    if before:
                        pe.wait_ge(sum_d, upto(dve_sums, before[-1]))
                        pe.wait_ge(saved, upto(act_saves, before[-1]))
                    else:
                        pe.wait_ge(h_saved, ZEROED + (FUSED - 1) * NB)
                if need >= 0:
                    need_row(need)
                if s == 0 and kind == "single":
                    pe.wait_ge(col_ready, COLS - min(LEFT[-1] - j, len(LEFT)))
                if stays(j):
                    block_of = lambda a: kept[:, i, a, :]
                else:
                    slot, loads = places[u, m]
                    if (u, m) not in HELD:
                        pe.wait_ge(loaded[slot], 16 * (loads_of(FUSED, 0, 0) + loads))
                    block_of = lambda a: ring[:, slot, a, :]
                if kind == "single":
                    ins = single(single_bank_of(u), lambda a: ops[:, SUB * j + a, half], block_of,
                                 m == singles[0], m == singles[-1])
                else:
                    for a in range(SUB):
                        ins = nc.tensor.matmul(bank[PAIR_BANK + u % 2][:, :], ops[:, SUB * j + a, :],
                                               block_of(a), start=m == pairs[0] and a == 0,
                                               stop=m == pairs[-1] and a == SUB - 1)
                if m == len(row) - 1:
                    ins.then_inc(row_done, 1)
                elif both(u) and m == singles[-1]:
                    ins.then_inc(singles_done, 1)
                elif not stays(j):
                    ins.then_inc(blocks_used, 1)
                if (u, m) in LAST_H:
                    add_h(FUSED - 1, LAST_H.index((u, m)), TURN_BANK)
                if project_now:
                    project(project_now[-1])
                    project_now = []
            turn_last(UNITS)

        @block.scalar
        def _(act):
            def copy(to, src):
                return nc.scalar.activation(to, src, ACT.Copy)

            def column_out(lane, done, at, turned):
                act.wait_ge(done, at)
                if turned is not None:
                    act.wait_ge(col_turned, turned)
                copy(sums[:, lane, :], bank[lane][:, :]).then_inc(col_out, 1)

            def keep(b, before):
                for k in range(SUB):
                    act.wait_ge(slice_turned, before + k + 1)
                    copy(kept[:, b, k, :], bank[TURN_BANK + k % 2][:, :]).then_inc(slice_kept, 1)

            for b in range(NB):
                if b == NB - 1:
                    column_out(0, fused_done, 1, None)
                if by_pe_first(b):
                    keep(b, SUB * turned_before_first(b))

            def turn(q):
                for b in range(NB - 1):
                    if by_pe(b):
                        keep(b, SUB * turned_before(q, b))
                for lane, (done, at) in enumerate(((fused_done, q + 1), (plain_used, plain_count(q, NB - 1)))):
                    column_out(lane, done, at, turned_count(q, 0) - 1)
                keep(NB - 1, SUB * turned_before(q, NB - 1))

            with act.Fori(1, FUSED) as q:
                turn(q)
            column_out(0, plain_used, ALL_PLAIN + NB, ALL_OUT)

            def feats(u):
                for v in projections_in(u):
                    w = projection(v)
                    act.wait_ge(pair_turned, w + 1)
                    if w:
                        act.wait_ge(proj_done, w)
                    copy(feat[:, :], bank[TURN_BANK][:, :]).then_inc(feat_ready, 1)

            def store(v):
                i = row_of(v)[1]
                act.wait_ge(result_ready, v - 3 * NB + 1)
                act.dma_start(out[:, SUB * i:SUB * (i + 1), :], result[v % 2][:, :, :]).then_inc(stored[v % 2], 16)

            for u in range(UNITS):
                s, i = row_of(u)
                feats(u)
                if u >= 3 * NB + 2:
                    store(u - 2)
                if both(u):
                    act.wait_ge(singles_done, upto(both, u))
                else:
                    act.wait_ge(row_done, u + 1)
                if u < 2:
                    act.wait_ge(col_turned, COLS)
                else:
                    act.wait_ge(row_turned, u - 1)
                single_bank, pair_bank = bank[single_bank_of(u)], bank[PAIR_BANK + u % 2]
                into = sums[:, u % 2, :]
                if act_sums(u):
                    if s == 0:
                        act.wait_ge(h_saved, h_before(i))
                        ins = copy(into[HI], save[HI, i, :])
                    elif s == 1:
                        ins = copy(into[LO], single_bank[LO, :])
                    elif s == 2:
                        ins = copy(into[HI], single_bank[HI, :])
                    elif i:
                        ins = copy(into[LO], single_bank[LO, :])
                    else:
                        ins = copy(into, single_bank[:, :])
                    ins.then_inc(sum_a, 1)
                if act_saves(u):
                    act.wait_ge(row_done, u + 1)
                    act.wait_ge(sum_d, upto(dve_sums, u))
                    if upto(act_sums, u):
                        act.wait_ge(sum_a, upto(act_sums, u))
                    half = LO if s == 1 else HI
                    copy(save[half, i, :], pair_bank[half, :]).then_inc(saved, 1)
            store(UNITS - 2)
            store(UNITS - 1)
            for n in range(2):
                act.wait_ge(stored[n], 16 * NB // 2)

        @block.vector
        def _(dve):
            steps = Steps(dve, dve_step)
            link = steps.link
            add = lambda to, a, b: nc.vector.tensor_tensor(to, a, b, ALU.add)
            mul = lambda to, a, b: nc.vector.tensor_tensor(to, a, b, ALU.mult)

            def over_rows(v, n=SUB):
                return v.unsqueeze(1).to_broadcast([P, n, D])

            dve.wait_ge(inputs_in, 16 * INPUTS)
            mul(coef[:, 0:1], par_sb[:, 0:1], par_sb[:, 1:2])
            link(mul(coef[:, 1:2], par_sb[:, 2:3], par_sb[:, 3:4]))
            for n, part in enumerate((diag_sb[:, 0:USERS // P], diag_sb[:, USERS // P:])):
                ins = nc.vector.tensor_scalar(part, part, coef[:, n:n + 1], None, ALU.mult)
            link(ins)
            for g in range(GROUPS):
                if g < 2:
                    dve.wait_ge(x_in[g], 16)
                dve.wait_ge(xw_done, g + 1)
                for n in range(2):
                    at = SUB * (g + GROUPS * n)
                    part = slice(at, at + SUB)
                    product = bank[group_bank(g)][:, :].rearrange("p (a f) -> p a f", f=2 * D)
                    link(mul(work[:, :, :], product[:, :, (LO, HI)[n]],
                             diag_sb[:, part].unsqueeze(2).to_broadcast([P, SUB, D])))
                    add(ops[:, part, HI], work[:, :, :], acc[:, part, :]).then_inc(e_ready, 1)
                    dve.wait_ge(e_ready, 2 * g + n + 1)
            def halves(n):
                v = bank[n][:, :].rearrange("p (a f) -> p a f", f=2 * D)
                return v[:, :, LO], v[:, :, HI]

            def fold_column(count, col, fused):
                dve.wait_ge(col_turned, count)
                low, high = halves(COL_BANK)
                link(nc.vector.tensor_copy(tmp[:, :, :], high))
                if fused:
                    add(pfused[:, :, :], low, tmp[:, :, :])
                add(ops[:, bass.ds(SUB * col, SUB), LO], low, tmp[:, :, :]).then_inc(col_ready, 1)
                dve.wait_ge(col_ready, count)

            def save_h(q, b, source=PAIR_BANK):
                dve.wait_ge(h_done, NB * q + b + 1)
                dve.wait_ge(h_saved, ZEROED + NB * q + b)
                add(save[:, b, :], bank[source + b % 2][:, :], save[:, b, :]).then_inc(h_saved, 1)

            def turn_squares(b, slot, loads, rows):
                src = ring[:, slot].rearrange("p a (k c) -> p a k c", c=P)
                dst = kept[:, b].rearrange("p k (a c) -> p a k c", c=P)
                dve.wait_ge(loaded[slot], 16 * loads)
                for r in rows:
                    for c in range(P // 32):
                        part_r, part_c = slice(32 * r, 32 * r + 32), slice(32 * c, 32 * c + 32)
                        ins = nc.vector.transpose(dst[part_c, :, :, part_r], src[part_r, :, :, part_c])
                return ins

            def start_squares(q, b, rows=(0, 1)):
                turn_squares(b, slot_of(b, 0), loads_of(q, b, 0), rows)

            def finish_squares(q, b, rows=(2, 3)):
                dve.wait_ge(plain_used, plain_count(q, b))
                turn_squares(b, slot_of(b, 0), loads_of(q, b, 0), rows).then_inc(block_kept, 1)

            last = max(b for b in range(NB) if not by_pe_first(b))
            for b in range(NB):
                if not by_pe_first(b):
                    turn_squares(b, b, 1, (0, 1))
                    if b == last:
                        fold_column(1, PLAIN, True)
                    turn_squares(b, b, 1, (2, 3)).then_inc(block_kept, 1)

            def turn(q):
                for b in range(NB):
                    if b:
                        save_h(q - 1, b - 1)
                    if b % 2:
                        start_squares(q, b - 1, (0, 1) if b < NB - 1 else (0,))
                    elif b:
                        finish_squares(q, b - 2)
                save_h(q - 1, NB - 1)
                fold_column(turned_count(q, 0), PLAIN + q, True)
                fold_column(turned_count(q, 1), q - 1, False)
                finish_squares(q, NB - 2, (1, 2, 3))

            done, per = steps.n, LANES
            with dve.Fori(1, FUSED) as q:
                steps.base, steps.n = done + per * (q - 1), 0
                turn(q)
                assert steps.n == per
            steps.base, steps.n = 0, done + per * (FUSED - 1)
            nc.vector.scalar_tensor_tensor(acc[:, :, :], acc[:, :, :], 2.0, over_rows(beta_sb, TILES),
                                           ALU.mult, ALU.add).then_inc(weights_ready, 1)
            dve.wait_ge(const_step, 3)
            for half in (LO, HI):
                nc.vector.tensor_tensor(w_pair[:, half], w10_in, w32_in, ALU.subtract)
                nc.vector.tensor_scalar(w_w[:, half], w33_in, 2.0, None, ALU.mult)
            nc.vector.tensor_scalar(w_z[:, HI], w22_in, 2.0, None, ALU.mult)
            add(w_z[:, LO], ident[:, LO], ident[:, HI]).then_inc(weights_ready, 1)
            for b in range(NB):
                if LAST_H[b][0] == "left":
                    save_h(FUSED - 1, b, TURN_BANK)
            fold_column(COLS, LEFT[0], False)

            dve.wait_ge(weights_ready, 1)
            norms = 0

            def norm(to, src):
                nonlocal norms
                norms += 1
                for a in range(SUB):
                    ins = nc.vector.bn_stats(stats[:, a, :], src[:, a, :])
                link(ins)
                for a in range(SUB):
                    ins = nc.vector.bn_aggr(mv[:, a, :], stats[:, a, :])
                link(ins)
                nc.vector.tensor_scalar(veps[:, :], mv[:, :, 1], EPS, None, ALU.add).then_inc(var_ready, 1)
                dve.wait_ge(rstd_ready, norms)
                for a in range(SUB):
                    ins = nc.vector.tensor_scalar(to[:, a, :], src[:, a, :], mv[:, a, 0:1], rstd[:, a:a + 1],
                                                  ALU.subtract, ALU.mult)
                return ins

            def use_projection(v):
                w, i = projection(v), row_of(v)[1]
                rows = slice(SUB * i, SUB * (i + 1))
                dve.wait_ge(proj_done, w + 1)
                link(add(acc[:, rows, :], halves(PROJ_BANK)[0], over_rows(bias_sb)))
                add(acc[:, rows, :], acc[:, rows, :], ops[:, rows, HI]).then_inc(proj_used, 1)
                dve.wait_ge(proj_used, w + 1)

            for u in range(UNITS):
                s, i = row_of(u)
                rows = slice(SUB * i, SUB * (i + 1))
                for b in range(NB):
                    if LAST_H[b][0] == u:
                        save_h(FUSED - 1, b, TURN_BANK)
                if both(u):
                    dve.wait_ge(singles_done, upto(both, u))
                else:
                    dve.wait_ge(row_done, u + 1)
                if u < 2:
                    dve.wait_ge(col_turned, COLS)
                else:
                    dve.wait_ge(row_turned, u - 1)
                single_bank, pair_bank = bank[single_bank_of(u)], bank[PAIR_BANK + u % 2]
                into = sums[:, u % 2, :]
                if dve_sums(u):
                    end = (LO, HI, LO, HI)[s]
                    part = slice(0, P) if s == 0 and i < PLAIN else end
                    if s == 0:
                        dve.wait_ge(h_saved, h_before(i))
                        found = True
                        first = pair_bank[LO, :] if i >= PLAIN else single_bank[:, :]
                    else:
                        found = (s == 1 and i > 0) or (s == 2 and i < NB - 1) or s == 3
                        first = single_bank[part, :]
                        if found:
                            dve.wait_ge(saved, upto(act_saves, unit_of(s - 1, i)))
                    if found:
                        ins = add(into[part], first, save[part, i, :])
                    else:
                        ins = nc.vector.tensor_copy(into[part], first)
                    if both(u):
                        link(ins)
                        dve.wait_ge(row_done, u + 1)
                        ins = add(into[end], pair_bank[end, :], into[end])
                    ins.then_inc(sum_d, 1)
                dve.wait_ge(row_turned, u + 1)
                low, high = halves(single_bank_of(u))
                t0, sum_of = ops[:, rows, HI], acc[:, rows, :]
                if s < 2:
                    link(nc.vector.tensor_copy(tmp[:, :, :], high))
                if s == 0:
                    v = work[:, :, :]
                    link(add(v, low, tmp[:, :, :]))
                    link(norm(v, v))
                    link(mul(v, v, over_rows(gamma_sb)))
                    link(add(v, v, sum_of))
                    norm(t0, v).then_inc(row_ready, 1)
                elif s == 1:
                    add(ops[:, rows, LO], low, tmp[:, :, :]).then_inc(row_ready, 1)
                elif s == 2:
                    add(sum_of, high, sum_of)
                    nc.vector.scalar_tensor_tensor(t0, low, 2.0, t0, ALU.mult, ALU.subtract
                                                   ).then_inc(row_ready, 1)
                else:
                    add(work[:, :, :], high, sum_of).then_inc(row_ready, 1)
                    if u > 3 * NB + 1:
                        dve.wait_ge(stored[u % 2], 16 * ((u - 3 * NB) // 2))
                dve.wait_ge(row_ready, u + 1)
                if s == 3:
                    norm(result[u % 2], work).then_inc(result_ready, 1)
                    dve.wait_ge(result_ready, u - 3 * NB + 1)
                for v in projections_in(u + 1):
                    use_projection(v)

        @block.gpsimd
        def _(pool):
            nc.gpsimd.memset(minus_half[:, :], -0.5).then_inc(const_step, 1)
            nc.gpsimd.memset(ident[:, :], 0.0).then_inc(const_step, 1)
            pool.wait_ge(const_step, 2)
            nc.gpsimd.affine_select(out=ident[:, :], in_=ident[:, :], compare_op=ALU.not_equal, fill=1.0,
                                    base=0, pattern=[[-1, P]], channel_multiplier=1).then_inc(const_step, 1)
            pool.wait_ge(xw_done, GROUPS)
            for part in (slice(0, NB // 2), slice(NB // 2, NB)):
                nc.gpsimd.memset(save[:, part, :], 0.0).then_inc(h_saved, 1)
            with pool.Fori(0, NORMS) as n:
                pool.wait_ge(var_ready, n + 1)
                nc.gpsimd.tensor_tensor(rstd[:, :], veps[:, :], minus_half[:, :], ALU.pow).then_inc(rstd_ready, 1)


def kernel(x, adj, L0_gnn_W_u, L0_gnn_diag_u, L0_gnn_par_u, L0_gnn_W_i, L0_gnn_diag_i, L0_gnn_par_i,
           L0_gnn_ln_gamma, L0_gnn_ln_beta, L1_gnn_weights, L1_gnn_bias):
    import concourse.bacc as bacc
    from concourse.bass_utils import run_bass_kernel_spmd

    nc = bacc.Bacc("TRN2", target_bir_lowering=False, num_devices=1, dynamic_dma_scratch_size=1024)
    lay = np.ascontiguousarray
    x, adj, W_u, W_i, W = (np.asarray(v) for v in (x, adj, L0_gnn_W_u, L0_gnn_W_i, L1_gnn_weights))

    none = np.zeros_like(W_u)

    def blocks(m):
        return lay(m.reshape(NB, SUB, P, NB, BLK).transpose(3, 0, 2, 1, 4)).reshape(NB * NB, P, SUB * BLK)

    def by_partition(v):
        return lay(v.reshape(-1, P).T)

    arrays = {
        "a_nat": blocks(adj), "a_tr": blocks(adj.T),
        "x": lay(x.reshape(TILES, P, D).transpose(1, 0, 2)),
        "xT": lay(x.reshape(2, N // 2, D).transpose(0, 2, 1)).reshape(P, N // 2),
        "diag": by_partition(np.concatenate([L0_gnn_diag_u, L0_gnn_diag_i])),
        "rows": np.concatenate([L0_gnn_ln_gamma, L0_gnn_ln_beta, L1_gnn_bias, L0_gnn_par_u, L0_gnn_par_i]),
        "weights": lay(np.concatenate([np.concatenate(over) for over in (
            (W_u, none), (none, W_i), (W_i, none), (none, W_i),
            (W[1], W[0]), (W[3], W[2]), (W[2], W[2]), (W[3], W[3]))], axis=1)),
    }
    t = {name: nc.dram_tensor(name, a.shape, F32, kind="ExternalInput").ap() for name, a in arrays.items()}
    out = nc.dram_tensor("out", (P, TILES, D), F32, kind="ExternalOutput").ap()
    build(nc, t["a_nat"], t["a_tr"], t["x"], t["xT"], t["diag"], t["rows"], t["weights"], out)
    r = run_bass_kernel_spmd(nc, [arrays], core_ids=[0])
    return lay(r.results[0]["out"].transpose(1, 0, 2)).reshape(N, D)
```
